# Optimizing a Trainium2 kernel written in Bass

```python
import numpy as np
import jax
import jax.numpy as jnp

def _softmax(x, axis=-1):
    return jax.nn.softmax(x, axis=axis)

def _gelu(x):
    return jax.nn.gelu(x, approximate=True)

def _silu(x):
    return jax.nn.silu(x)

def _sigmoid(x):
    return jax.nn.sigmoid(x)

def _layernorm(x, axis=-1, eps=1e-05):
    m = jnp.mean(x, axis=axis, keepdims=True)
    v = jnp.var(x, axis=axis, keepdims=True)
    return (x - m) / jnp.sqrt(v + eps)

def _scatter_add(tgt, idx, src, axis=0):
    return tgt.at[idx].add(src)

def _segment_sum(src, seg, n):
    return jax.ops.segment_sum(src, seg, n)
kernel_name = 'mk_macaron_d2_jaxref_r8_038523'

def setup_inputs(seed: int=0):
    np.random.seed(seed)
    _w = jnp.asarray

    def _L0_attn_setup():
        import jax, jax.numpy as jnp
        import numpy as np
        HEADS = 16
        key = jax.random.key(seed)
        k1, k2, k3 = jax.random.split(key, 3)
        b, n, c = (4, 512, 128)
        x = jax.random.normal(k1, (b, n, c), dtype=jnp.float32)
        qkv_w = jax.random.normal(k2, (c, c), dtype=jnp.float32) * c ** (-0.5)
        temp = jnp.ones((HEADS, 1), dtype=jnp.float32)
        out_w = jax.random.normal(k3, (c, c), dtype=jnp.float32) * c ** (-0.5)
        out_b = jnp.zeros((c,), dtype=jnp.float32)
        return {'x': x, 'qkv_w': qkv_w, 'temp': temp, 'out_w': out_w, 'out_b': out_b}
    _L0_attn_in = _L0_attn_setup()

    def _L0_ffn_setup():
        import jax, jax.numpy as jnp
        import numpy as np
        D_MODEL = 128
        D_FF = 512
        N_EXPERTS = 4
        key = jax.random.key(seed)
        ks = jax.random.split(key, 8)
        s_in = 1.0 / np.sqrt(D_MODEL)
        s_ff = 1.0 / np.sqrt(D_FF)
        x = jax.random.normal(ks[0], (4, 256, D_MODEL), dtype=jnp.float32)
        W1 = jax.random.uniform(ks[1], (N_EXPERTS, D_MODEL, D_FF), jnp.float32, -s_in, s_in)
        b1 = jax.random.uniform(ks[2], (N_EXPERTS, D_FF), jnp.float32, -s_in, s_in)
        W2 = jax.random.uniform(ks[3], (N_EXPERTS, D_FF, D_MODEL), jnp.float32, -s_ff, s_ff)
        b2 = jax.random.uniform(ks[4], (N_EXPERTS, D_MODEL), jnp.float32, -s_ff, s_ff)
        Wg = jax.random.uniform(ks[5], (D_MODEL, N_EXPERTS), jnp.float32, -s_in, s_in)
        bg = jax.random.uniform(ks[6], (N_EXPERTS,), jnp.float32, -s_in, s_in)
        return {'x': x, 'W1': W1, 'b1': b1, 'W2': W2, 'b2': b2, 'Wg': Wg, 'bg': bg}
    _L0_ffn_in = _L0_ffn_setup()

    def _L1_attn_setup():
        import jax, jax.numpy as jnp
        import numpy as np
        NUM_HEADS = 16
        ROPE_BASE = 10000.0
        ROPE_SCALE = 3.0

        def _rope_tables(L, head_dim, dtype):
            theta = 1.0 / ROPE_BASE ** (jnp.arange(0, head_dim, 2, dtype=jnp.float32) / head_dim) * ROPE_SCALE
            ang = jnp.arange(L, dtype=jnp.float32)[:, None] * theta[None, :]
            return (jnp.cos(ang).astype(dtype), jnp.sin(ang).astype(dtype))

        def _apply_rope(t, cos, sin):
            B, H, L, D = t.shape
            tr = t.reshape(B, H, L, D // 2, 2)
            real, imag = (tr[..., 0], tr[..., 1])
            c = cos[None, None, :, :]
            s = sin[None, None, :, :]
            out_real = real * c - imag * s
            out_imag = real * s + imag * c
            return jnp.stack([out_real, out_imag], axis=-1).reshape(B, H, L, D)
        key = jax.random.key(seed)
        k1, k2, k3 = jax.random.split(key, 3)
        B, L, C = (4, 256, 128)
        std = 1.0 / np.sqrt(C)
        x = jax.random.normal(k1, (B, L, C), dtype=jnp.float32)
        w_qkv = jax.random.normal(k2, (C, 3 * C), dtype=jnp.float32) * std
        w_proj = jax.random.normal(k3, (C, C), dtype=jnp.float32) * std
        b_proj = jnp.zeros((C,), dtype=jnp.float32)
        return {'x': x, 'w_qkv': w_qkv, 'w_proj': w_proj, 'b_proj': b_proj}
    _L1_attn_in = _L1_attn_setup()

    def _L1_ffn_setup():
        import jax, jax.numpy as jnp
        import numpy as np
        DMODEL = 128
        N_EXPERTS = 32
        EXPERT_SIZE = 64
        N_HEADS = 4
        WEIGHT_SCALE = 1.0
        key = jax.random.key(seed)
        k0, k1, k2, k3 = jax.random.split(key, 4)
        x = jax.random.normal(k0, (2, 256, DMODEL), dtype=jnp.float32)
        expert_sel = jax.random.normal(k1, (N_EXPERTS, DMODEL), dtype=jnp.float32) * DMODEL ** (-0.5)
        keys = jax.random.normal(k2, (N_EXPERTS, DMODEL, EXPERT_SIZE), dtype=jnp.float32) * DMODEL ** (-0.5)
        values = jax.random.normal(k3, (N_EXPERTS, EXPERT_SIZE, DMODEL), dtype=jnp.float32) * (N_EXPERTS * EXPERT_SIZE) ** (-0.5)
        return {'x': x, 'expert_sel': expert_sel, 'keys': keys, 'values': values}
    _L1_ffn_in = _L1_ffn_setup()
    _d = {'L0_attn_x': _L0_attn_in['x'], 'L0_attn_qkv_w': _L0_attn_in['qkv_w'], 'L0_attn_temp': _L0_attn_in['temp'], 'L0_attn_out_w': _L0_attn_in['out_w'], 'L0_attn_out_b': _L0_attn_in['out_b'], 'L0_ffn_W1': _L0_ffn_in['W1'], 'L0_ffn_b1': _L0_ffn_in['b1'], 'L0_ffn_W2': _L0_ffn_in['W2'], 'L0_ffn_b2': _L0_ffn_in['b2'], 'L0_ffn_Wg': _L0_ffn_in['Wg'], 'L0_ffn_bg': _L0_ffn_in['bg'], 'L1_attn_w_qkv': _L1_attn_in['w_qkv'], 'L1_attn_w_proj': _L1_attn_in['w_proj'], 'L1_attn_b_proj': _L1_attn_in['b_proj'], 'L1_ffn_expert_sel': _L1_ffn_in['expert_sel'], 'L1_ffn_keys': _L1_ffn_in['keys'], 'L1_ffn_values': _L1_ffn_in['values']}
    _x0 = _d['L0_attn_x']
    _d['L0_attn_x'] = jax.random.normal(jax.random.fold_in(jax.random.key(seed), 1), (16, 512, 128), dtype=_x0.dtype)
    del _x0
    return _d

def reference(L0_attn_x, L0_attn_qkv_w, L0_attn_temp, L0_attn_out_w, L0_attn_out_b, L0_ffn_W1, L0_ffn_b1, L0_ffn_W2, L0_ffn_b2, L0_ffn_Wg, L0_ffn_bg, L1_attn_w_qkv, L1_attn_w_proj, L1_attn_b_proj, L1_ffn_expert_sel, L1_ffn_keys, L1_ffn_values):

    def _L0_attn_ref(x, qkv_w, temp, out_w, out_b):
        import jax, jax.numpy as jnp
        import numpy as np
        HEADS = 16
        b, n, c = x.shape
        h = HEADS
        d = c // h
        w = jnp.einsum('bnc,oc->bno', x, qkv_w).reshape(b, n, h, d).transpose(0, 2, 1, 3)
        norm = jnp.sqrt(jnp.sum(w * w, axis=-2, keepdims=True))
        w_normed = w / jnp.maximum(norm, 1e-12)
        s = jnp.sum(w_normed * w_normed, axis=-1) * temp[None, :, :]
        pi = jax.nn.softmax(s, axis=1)
        pi_norm = pi / (jnp.sum(pi, axis=-1, keepdims=True) + 1e-08)
        dots = jnp.einsum('bhn,bhnd->bhd', pi_norm, w * w)
        attn = 1.0 / (1.0 + dots)
        out = -w * pi[..., None] * attn[:, :, None, :]
        out = out.transpose(0, 2, 1, 3).reshape(b, n, c)
        return jnp.einsum('bnc,oc->bno', out, out_w) + out_b

    def _L0_ffn_ref(x, W1, b1, W2, b2, Wg, bg):
        import jax, jax.numpy as jnp
        import numpy as np
        D_MODEL = 128
        D_FF = 512
        N_EXPERTS = 4
        gate_logits = jnp.einsum('bld,de->ble', x, Wg) + bg
        idx = jnp.argmax(jax.nn.softmax(gate_logits, axis=-1), axis=-1)
        h = jnp.einsum('bld,edf->belf', x, W1) + b1[None, :, None, :]
        h = jax.nn.gelu(h, approximate=False)
        y = jnp.einsum('belf,efd->beld', h, W2) + b2[None, :, None, :]
        onehot = jax.nn.one_hot(idx, N_EXPERTS, dtype=x.dtype)
        out = jnp.einsum('beld,ble->bld', y, onehot)
        return out

    def _L1_attn_ref(x, w_qkv, w_proj, b_proj):
        import jax, jax.numpy as jnp
        import numpy as np
        NUM_HEADS = 16
        ROPE_BASE = 10000.0
        ROPE_SCALE = 3.0

        def _rope_tables(L, head_dim, dtype):
            theta = 1.0 / ROPE_BASE ** (jnp.arange(0, head_dim, 2, dtype=jnp.float32) / head_dim) * ROPE_SCALE
            ang = jnp.arange(L, dtype=jnp.float32)[:, None] * theta[None, :]
            return (jnp.cos(ang).astype(dtype), jnp.sin(ang).astype(dtype))

        def _apply_rope(t, cos, sin):
            B, H, L, D = t.shape
            tr = t.reshape(B, H, L, D // 2, 2)
            real, imag = (tr[..., 0], tr[..., 1])
            c = cos[None, None, :, :]
            s = sin[None, None, :, :]
            out_real = real * c - imag * s
            out_imag = real * s + imag * c
            return jnp.stack([out_real, out_imag], axis=-1).reshape(B, H, L, D)
        B, L, C = x.shape
        H = NUM_HEADS
        D = C // H
        scale = D ** (-0.5)
        qkv = (x @ w_qkv).reshape(B, L, 3, H, D).transpose(2, 0, 3, 1, 4)
        q, k, v = (qkv[0], qkv[1], qkv[2])
        cos, sin = _rope_tables(L, D, x.dtype)
        q = _apply_rope(q, cos, sin)
        k = _apply_rope(k, cos, sin)
        attn = jnp.einsum('bhqd,bhkd->bhqk', q, k) * scale
        attn = jax.nn.softmax(attn, axis=-1)
        out = jnp.einsum('bhqk,bhkd->bhqd', attn, v)
        out = out.transpose(0, 2, 1, 3).reshape(B, L, C)
        return out @ w_proj + b_proj

    def _L1_ffn_ref(x, expert_sel, keys, values):
        import jax, jax.numpy as jnp
        import numpy as np
        DMODEL = 128
        N_EXPERTS = 32
        EXPERT_SIZE = 64
        N_HEADS = 4
        WEIGHT_SCALE = 1.0
        B, S, D = x.shape
        xt = x.reshape(-1, D)
        N = xt.shape[0]
        sel_logits = jnp.einsum('nd,ed->ne', xt, expert_sel)
        gates = jax.nn.sigmoid(sel_logits)
        sel_val, sel_idx = jax.lax.top_k(gates, N_HEADS)
        gate_full = jnp.zeros_like(gates).at[jnp.arange(N)[:, None], sel_idx].set(sel_val)
        scores = jax.nn.relu(jnp.einsum('nd,edf->nef', xt, keys))
        scores = scores * gate_full[:, :, None]
        out = jnp.einsum('nef,efv->nv', scores, values)
        return out.reshape(B, S, -1)
    x = L0_attn_x
    x = x + 0.5 * _L0_ffn_ref(_layernorm(x, axis=-1), L0_ffn_W1, L0_ffn_b1, L0_ffn_W2, L0_ffn_b2, L0_ffn_Wg, L0_ffn_bg)
    x = x + _L0_attn_ref(_layernorm(x, axis=-1), L0_attn_qkv_w, L0_attn_temp, L0_attn_out_w, L0_attn_out_b)
    x = x + 0.5 * _L0_ffn_ref(_layernorm(x, axis=-1), L0_ffn_W1, L0_ffn_b1, L0_ffn_W2, L0_ffn_b2, L0_ffn_Wg, L0_ffn_bg)
    x = x + 0.5 * _L1_ffn_ref(_layernorm(x, axis=-1), L1_ffn_expert_sel, L1_ffn_keys, L1_ffn_values)
    x = x + _L1_attn_ref(_layernorm(x, axis=-1), L1_attn_w_qkv, L1_attn_w_proj, L1_attn_b_proj)
    x = x + 0.5 * _L1_ffn_ref(_layernorm(x, axis=-1), L1_ffn_expert_sel, L1_ffn_keys, L1_ffn_values)
    return x

_drawn_inputs = setup_inputs


def setup_inputs(seed=0):
    import zlib

    import numpy as np

    out = dict(_drawn_inputs(seed))
    spreads = {'L0_attn_temp': (1.0, 0.2), 'L0_attn_out_b': (0.0, 0.1), 'L1_attn_b_proj': (0.0, 0.1)}
    factors = {}
    for name, (base, spread) in spreads.items():
        noise = np.random.default_rng([zlib.crc32(name.encode()), seed]).standard_normal(out[name].shape)
        drawn = base * np.exp(spread * noise) if base else spread * noise
        out[name] = jnp.asarray(drawn.astype(out[name].dtype))
    for name, factor in factors.items():
        out[name] = (out[name] * factor).astype(out[name].dtype)
    return out
```

```python
from contextlib import ExitStack

import numpy as np

import concourse.bass as bass
from concourse import mybir

ALU = mybir.AluOpType
ACT = mybir.ActivationFunctionType
AXX = mybir.AxisListType.X
F32 = mybir.dt.float32
F32R = mybir.dt.float32r
BF16 = mybir.dt.bfloat16
FP16 = mybir.dt.float16

P = 128
D = 128
BATCH, SEQ = 16, 512
BLK = SEQ // P
TILES = BATCH
PAIRS = TILES // 2
HEADS, HD = 16, 8
E0, FF0 = 4, 512
FB0 = FF0 // P
E1, FF1 = 32, 64
FB1 = E1 * FF1 // P
PER1 = P // FF1
TOP1 = 4
LEAD = 3
BIG = 3.0e38
LN_EPS = 1e-5
GROUPS, HPG = 4, 4
VC = 3 * HD + 1
SCALE = HD ** -0.5
POOL_FB = (2, 5, 8, 11, 14)
POOL_KB = 2
AHEAD = 5
EARLY = 3
FIRST = (0, 0, TILES, 0, 0, TILES)
KIND = (0, 1, 0, 3, 4, 3)
HP = 2


def token_constants():
    c = {}
    c["ident"] = np.eye(P, dtype=np.float32)
    s = np.zeros((P, E0, P), np.float32)
    for e in range(E0):
        s[e, e, :] = 1
    c["sel_expert"] = s.reshape(P, -1)
    s = np.zeros((P, FB1, P), np.float32)
    for part in range(3):
        for e in range(E1):
            s[part * E1 + e, e // PER1, (e % PER1) * FF1:(e % PER1 + 1) * FF1] = 1
    c["sel_gate"] = s.reshape(P, -1)
    small = np.zeros((P, 64), np.float32)
    small[0:4, 0] = small[4:8, 1] = small[8:12, 2] = 1
    small[0, 3] = small[1, 4] = small[2, 5] = 1
    small[:, 6:10] = [4, 3, 2, 1]
    for j in range(HPG):
        small[32 * j + 3 * HD, 10] = 1
    for ch in range(P):
        small[ch, 16 + ch // HD] = 1
    small[0:3, 11] = 1
    c["small"] = small
    s = np.zeros((P, P), np.float32)
    for ch in range(P):
        s[ch // HD, ch] = 1
    c["head_rows"] = s
    s = np.zeros((P, GROUPS, 4, P), np.float32)
    for g in range(GROUPS):
        for j in range(HPG):
            for d in range(HD):
                ch, r = (HPG * g + j) * HD + d, 32 * j + d
                s[ch, g, 0, r] = s[ch, g, 0, r + HD] = 1
                s[ch, g, 1, r + 2 * HD] = 1
                s[ch, g, 2, r] = s[ch, g, 2, r + 2 * HD] = 1
                s[ch, g, 3, r + HD] = 1
    c["stack"] = s.reshape(P, -1)
    theta = (np.float32(1.0) / np.float32(10000.0) ** (np.arange(0, HD, 2, dtype=np.float32) / np.float32(HD))
             * np.float32(3.0)).astype(np.float32)
    ang = (np.arange(SEQ, dtype=np.float32)[:, None] * theta[None, :]).astype(np.float32)
    cos, sin = np.cos(ang.astype(np.float64)), np.sin(ang.astype(np.float64))
    col = np.arange(SEQ)
    pos = BLK * (col % P) + col // P
    ch = np.arange(P) % HD
    sign = np.where(ch % 2 == 0, -1.0, 1.0)[:, None]
    c["cos"] = np.ascontiguousarray(cos[pos][:, ch // 2].T.astype(np.float32))
    c["sin"] = np.ascontiguousarray((sin[pos][:, ch // 2].T * sign).astype(np.float32))
    return c


def macaron(nc, x_in, w, const, out):
    whole = ExitStack()
    with whole:
        def sem(name):
            return whole.enter_context(nc.semaphore(name))

        def persistent(name, shape, dt=F32):
            return whole.enter_context(nc.sbuf_tensor(name, shape, dt))

        ps = whole.enter_context(nc.psum_tensor("ps", [P, 8, 512], F32))

        x = persistent("x", [P, TILES * BLK, D])
        ident = persistent("ident", [P, P])
        ident_b = persistent("ident_b", [P, P], BF16)
        small = persistent("small", [P, 64])
        neg_half = persistent("neg_half", [P, BLK])
        keys_hl = persistent("keys_hl", [P, 2, E1 * FF1], F32R)
        vals_hl = persistent("vals_hl", [P, 2, FB1, D], F32R)
        sel_gate = persistent("sel_gate", [P, FB1, P], BF16)
        router1 = persistent("router1", [P, E1])
        xn = persistent("xn", [P, BLK, D])
        xnT = persistent("xnT", [P, SEQ])
        xnT_hl = [persistent(f"xnT_hl{b}", [P, 2, SEQ], F32R) for b in range(2)]
        stats = persistent("stats", [P, BLK, 6])
        meanvar = persistent("meanvar", [P, BLK, 2])
        var_eps = persistent("var_eps", [P, BLK])
        rstd = persistent("rstd", [P, BLK])

        early = ExitStack()

        def early_sb(name, shape, dt=F32):
            return early.enter_context(nc.sbuf_tensor(name, shape, dt))

        stage = [early_sb(f"stage{b}", [P, 2048]) for b in range(2)]
        w1_hl = early_sb("w1_hl", [P, 2, E0, FF0], F32R)
        w2_hl = early_sb("w2_hl", [P, 2, FB0, E0 * D], F32R)
        sel_expert = early_sb("sel_expert", [P, E0, P], BF16)
        gate_w = early_sb("gate_w", [P, E0])
        gate_b = early_sb("gate_b", [P, E0])
        bias_m = early_sb("bias_m", [P, 2, 512], BF16)
        ones3 = early_sb("ones3", [P, P], BF16)
        logit = early_sb("logit", [P, BLK, E0])
        best = early_sb("best", [P, BLK])
        equal = early_sb("equal", [P, BLK, E0])
        first = early_sb("first", [P, BLK])
        onehot = early_sb("onehot", [P, BLK, 3 * E0], BF16)
        half_hot = [early_sb(f"half_hot{b}", [P, BLK, E0]) for b in range(2)]
        onehotT = [early_sb(f"onehotT{b}", [P, SEQ], BF16) for b in range(2)]
        qkv_f = early_sb("qkv_f", [P, 2, P])
        qkvT_hl = early_sb("qkvT_hl", [P, 2, P], F32R)
        out_b0 = early_sb("out_b0", [P, D])
        temp_b = early_sb("temp_b", [P, HEADS])
        temp_ind = early_sb("temp_ind", [P, HEADS])
        head_rows = early_sb("head_rows", [P, P])

        with ExitStack() as once_own:
            bias_f = once_own.enter_context(nc.sbuf_tensor("bias_f", [P, 2, 512], F32))
            bias_p = once_own.enter_context(nc.sbuf_tensor("bias_p", [P, 3, 2, 512], BF16))
            bias_r = once_own.enter_context(nc.sbuf_tensor("bias_r", [P, 2, 2, 512], F32))

        ffn0_own = ExitStack()

        def ffn0_sb(name, shape, dt=F32):
            return ffn0_own.enter_context(nc.sbuf_tensor(name, shape, dt))

        x_masked = [ffn0_sb(f"x_masked{b}", [P, E0, 2, SEQ], F32R) for b in range(2)]
        g32 = ffn0_sb("g32", [P, FB0, SEQ])
        g_hi = ffn0_sb("g_hi", [P, FB0, SEQ], F32R)
        g_lo = ffn0_sb("g_lo", [P, FB0, SEQ], F32R)
        ffn0_own.close()
        att0_own = ExitStack()

        def att0_sb(name, shape, dt=F32):
            return att0_own.enter_context(nc.sbuf_tensor(name, shape, dt))

        w32 = [att0_sb(f"w32_{b}", [P, SEQ]) for b in range(2)]
        wsq = [att0_sb(f"wsq{b}", [P, SEQ]) for b in range(2)]
        norm2 = att0_sb("norm2", [P, 1])
        inv2 = att0_sb("inv2", [P, 1])
        norm_ind = att0_sb("norm_ind", [P, HEADS])
        smax = att0_sb("smax", [P, BLK])
        sexp = att0_sb("sexp", [P, BLK, HEADS])
        ssum = att0_sb("ssum", [P, BLK])
        pi = [att0_sb(f"pi{b}", [P, BLK, P]) for b in range(2)]
        piT = att0_sb("piT", [P, SEQ])
        pi_rows = att0_sb("pi_rows", [P, SEQ])
        pi_sum = att0_sb("pi_sum", [P, 1])
        prod = att0_sb("prod", [P, SEQ])
        dots = att0_sb("dots", [P, 4])
        outT = att0_sb("outT", [P, SEQ])
        att0_own.close()
        early.close()

        def ffn1_memory():
            with ExitStack() as own:
                def sb(name, shape, dt=F32):
                    return own.enter_context(nc.sbuf_tensor(name, shape, dt))
                m = dict(
                    logit=sb("logit1", [P, BLK, E1]), top8=sb("top8", [P, BLK, 8]),
                    taken=sb("taken", [P, BLK, E1]), sig=sb("sig", [P, BLK, E1]),
                    gate=sb("gate", [P, BLK, E1]), rest=sb("rest", [P, 2, BLK, E1]),
                    parts=sb("parts", [P, BLK, 3 * E1], BF16),
                    gateT=[sb(f"gateT{b}", [P, SEQ], BF16) for b in range(2)],
                    relu=sb("relu", [P, 4, SEQ]), m32=sb("m32", [P, 4, SEQ]),
                    hi=sb("hi", [P, 4, SEQ], F32R), lo=sb("lo", [P, 4, SEQ], F32R),
                    yT=sb("yT", [P, SEQ]))
            return m

        ffn1_mem = ffn1_memory()

        late = ExitStack()

        def late_sb(name, shape, dt=F32):
            return late.enter_context(nc.sbuf_tensor(name, shape, dt))

        w_qk = late_sb("w_qk", [P, 4, 2, P], F32R)
        w_v = late_sb("w_v", [P, P])
        w_o = late_sb("w_o", [P, P])
        out_b1 = late_sb("out_b1", [P, D])
        stack_sel = late_sb("stack_sel", [P, GROUPS, 4, P], F32R)
        cos_t = late_sb("cos_t", [P, SEQ])
        sin_t = late_sb("sin_t", [P, SEQ])
        rope = late_sb("rope", [P, 3, SEQ])
        qk_hl = [late_sb(f"qk_hl{b}", [P, 2, 2, SEQ], F32R) for b in range(2)]
        ident_r = late_sb("ident_r", [P, P], F32R)
        k_pad = late_sb("k_pad", [P, HEADS, SEQ], F32R)
        q_st = late_sb("q_st", [P, 2, SEQ], F32R)
        q_sh = late_sb("q_sh", [P, 2, SEQ], F32R)
        qmax = late_sb("qmax", [P, 2, HPG, BLK])
        shift = late_sb("shift", [P, 2, BLK, P], F32R)
        with ExitStack() as once_own:
            stage_l = [once_own.enter_context(nc.sbuf_tensor(f"stage_l{b}", [P, 2048], F32)) for b in range(2)]
        prob = late_sb("prob", [P, HP, BLK, SEQ])
        prob_lo = late_sb("prob_lo", [P, HP, BLK, SEQ], FP16)
        v32 = late_sb("v32", [P, BLK, D])
        vrest = late_sb("vrest", [P, 2, BLK, D])
        v_parts = [late_sb(f"v_parts{b}", [P, BLK, HEADS, VC], BF16) for b in range(2)]
        o_sum = late_sb("o_sum", [P, HPG * BLK, HD])
        o_rcp = late_sb("o_rcp", [P, HPG * BLK])
        o_all = late_sb("o_all", [P, BLK, D])
        oT = late_sb("oT", [P, SEQ])
        late.close()

        x_first, x_rest, w_in, stage_free = sem("x_first"), sem("x_rest"), sem("w_in"), sem("stage_free")
        consts, setup = sem("consts"), sem("setup")
        phase_end = sem("phase_end")
        stored = sem("stored")
        signals = {}

        def sig(ph, name):
            ph = KIND[ph]
            if (ph, name) not in signals:
                signals[ph, name] = sem(f"{name}_{ph}")
            return signals[ph, name]

        class Chain:

            def __init__(self, eng, s, per_tile):
                self.eng, self.s, self.per, self.n, self.t = eng, s, per_tile, 0, 0

            def tile(self, t):
                assert self.n in (0, self.per), (self.n, self.per, self.s)
                self.t, self.n = t, 0

            def step(self, ins):
                self.n += 1
                return ins.then_inc(self.s, 1)

            def settle(self):
                self.eng.wait_ge(self.s, self.t * self.per + self.n)

            def settle_alone(self):
                pass_wait(self.eng, self.s, self.t * self.per + self.n)

        passed = {}

        def pass_wait(eng, s, value):
            if eng not in passed:
                passed[eng] = sem(f"passed{len(passed)}")
            eng.wait_ge(s, value)
            eng.sem_inc(passed[eng], 1)

        def over_tiles(eng, ph, head, body):
            t0 = FIRST[ph]
            head(t0, 0)
            with eng.Fori(t0 // 2, t0 // 2 + PAIRS - 1) as pair:
                body(pair * 2, 0, True)
                body(pair * 2 + 1, 1, True)
            body(t0 + TILES - 2, 0, True)
            body(t0 + TILES - 1, 1, False)

        def two_more(t):
            return not isinstance(t, int)

        def barrier(eng, n):
            eng.drain().then_inc(phase_end, 1)
            eng.wait_ge(phase_end, 4 * n)

        FFN0_PH, FFN1_PH = (0, 2), (3, 5)
        TR, SM = 0, 1
        MASK, H0, Y0 = 2, 4, 6
        G1, H1, Y1 = 2, 4, 7
        h1_banks = (4, 5, 6)
        WT, SC, PT, PR, YA = 1, 2, 3, 4, 5
        PASS1, PASS2, OB, MISC = 0, 2, 6, 7

        def prob_hi(s):
            return prob[:, s].bitcast(BF16).rearrange("p b (n two) -> p b n two", two=2)[:, :, :, 1]

        def wide(bank, rows=P, dt=F32):
            v = ps[0:rows, bank, :]
            return v if dt == F32 else v.bitcast(dt)

        def rows4(bank):
            return ps[:, bank, :].rearrange("p (b n) -> p b n", b=BLK)

        block = whole.enter_context(nc.Block())
        views = w

        staged = [(v, n) for v, n in views["staged"]]

        @block.sync
        def _(sp):
            xv = x_in.rearrange("t (p b) d -> p t b d", p=P)
            xs = x[:, :, :].rearrange("p (t b) d -> p t b d", b=BLK)
            sp.dma_start(ident[:], const["ident"]).then_inc(consts, 16)
            sp.dma_start(small[:], const["small"]).then_inc(consts, 16)
            sp.dma_start(xs[:, 0:2], xv[:, 0:2]).then_inc(x_first, 16)
            sp.dma_start(gate_w[:], views["gate_w"]).then_inc(consts, 16)
            sp.dma_start(gate_b[:], views["gate_b"].partition_broadcast(P)).then_inc(consts, 16)
            sp.wait_ge(setup, 1)
            for part in range(3):
                sp.dma_start(bias_f[E0 * part:E0 * part + E0, 0, :], views["b1"]).then_inc(consts, 16)
                sp.dma_start(bias_f[part:part + 1, 1, :], views["b2"]).then_inc(consts, 16)
            sp.dma_start(router1[:], views["router1"]).then_inc(consts, 16)
            sp.dma_start(qkv_f[:, 0, :], views["qkv_w"]).then_inc(consts, 16)
            sp.dma_start(qkv_f[:, 1, :], views["out_w"]).then_inc(consts, 16)
            sp.dma_start(out_b0[:], views["out_b0"].partition_broadcast(P)).then_inc(consts, 16)
            sp.dma_start(temp_b[:], views["temp"].partition_broadcast(P)).then_inc(consts, 16)
            sp.dma_start(head_rows[:], const["head_rows"]).then_inc(consts, 16)
            for n, (v, cols) in enumerate(staged):
                if n >= 2:
                    sp.wait_ge(stage_free, n - 1)
                sp.dma_start(stage[n % 2][:, 0:cols], v).then_inc(w_in, 16)
                sp.wait_ge(w_in, 16 * (n + 1))
                if n == 1:
                    sp.dma_start(xs[:, 2:TILES], xv[:, 2:TILES]).then_inc(x_rest, 16)
            sp.wait_ge(phase_end, 4 * 4)
            for n, (dst, src) in enumerate([
                    (w_v[:], views["w_v"]), (w_o[:], views["w_o"]),
                    (out_b1[:], views["out_b1"].partition_broadcast(P)),
                    (cos_t[:], const["cos"]), (sin_t[:], const["sin"])]):
                sp.dma_start(dst, src).then_inc(sig(4, "tables"), 16)
            for n, (v, cols) in enumerate(views["staged_late"]):
                m = n + len(staged)
                sp.dma_start(stage_l[n][:, 0:cols], v).then_inc(w_in, 16)
                sp.wait_ge(w_in, 16 * (m + 1))
            ov = out.rearrange("t (p b) d -> p t b d", p=P)
            with sp.Fori(0, TILES) as t:
                sp.wait_ge(sig(5, "x_done"), (t + TILES) * 4 + 4)
                sp.dma_start(ov[:, bass.ds(t, 1)], xs[:, bass.ds(t, 1)]).then_inc(stored, 16)
            sp.wait_ge(stored, 16 * TILES)

        @block.gpsimd
        def _(pool):
            pool.memset(neg_half[:], -0.5)
            pool.memset(ones3[:], 0.0)
            pool.memset(bias_f[:], 0.0).then_inc(setup, 1)
            for b in range(2):
                last = pool.memset(onehotT[b][:], 0.0)
            last.then_inc(setup, 1)

            def rstd_of(ph):
                def head(t, p):
                    ve = sig(ph, "var_eps")
                    pass_wait(pool, sig(ph, "meanvar"), t + 1)
                    pool.tensor_scalar(var_eps[:], meanvar[:, :, 1], LN_EPS, None, ALU.add).then_inc(ve, 1)
                    pool.wait_ge(ve, t + 1)
                    pool.tensor_tensor(rstd[:], var_eps[:], neg_half[:], ALU.pow).then_inc(sig(ph, "rstd"), 1)
                return head

            def low_parts(ph, m):
                def body(t, p, more):
                    for fb in range(FB1):
                        if fb in POOL_FB:
                            pool.wait_ge(sig(ph, "hi"), t * FB1 + fb + 1)
                            pool.tensor_tensor(m["lo"][:, fb % 4, :], m["m32"][:, fb % 4, :],
                                               m["hi"][:, fb % 4, :].bitcast(F32),
                                               ALU.subtract).then_inc(sig(ph, "lo_pool"), 1)
                        if fb == 0 and more:
                            rstd_of(ph)(t + 1, 1 - p)
                return body

            for ph in range(3):
                if ph == 1:
                    for b in range(2):
                        last = pool.memset(pi[b][:], 0.0)
                    last.then_inc(sig(1, "zeroed"), 1)
                with pool.Fori(FIRST[ph], FIRST[ph] + TILES) as t:
                    rstd_of(ph)(t, 0)
                barrier(pool, ph + 1)
            for ph in (3, 4, 5):
                if ph in FFN1_PH:
                    m = ffn1_mem
                    for b in range(2):
                        last = pool.memset(m["gateT"][b][:], 0.0)
                    last.then_inc(sig(ph, "zeroed"), 1)
                    over_tiles(pool, ph, rstd_of(ph), low_parts(ph, m))
                else:
                    pool.memset(shift[:].bitcast(F32), 0.0)
                    for b in range(2):
                        pool.memset(v_parts[b][:, :, :, VC - 1:VC], 1.0)
                    pool.memset(k_pad[:].bitcast(F32), 0.0).then_inc(sig(4, "zeroed"), 1)

                    def bias(t):
                        pool.wait_ge(sig(4, "xn"), t + 1)
                        xt = x[:, bass.ds(t * BLK, BLK), :]
                        pool.tensor_tensor(xt, xt, out_b1[:].unsqueeze(1).broadcast_to([P, BLK, D]),
                                           ALU.add).then_inc(sig(4, "biased"), 1)

                    def x_low(t, p):
                        pool.wait_ge(sig(4, "x_hi"), t + 1)
                        pool.tensor_tensor(xnT_hl[p][:, 1, :], xnT[:], xnT_hl[p][:, 0, :].bitcast(F32),
                                           ALU.subtract).then_inc(sig(4, "x_lo"), 1)

                    def rope_sum(t, a):
                        if a == 1:
                            pool.wait_ge(sig(4, "qk_hl"), t * 2 + 1)
                        pool.wait_ge(sig(4, "qk_read"), t * 4 + 2 * a + 2)
                        pool.tensor_tensor(rope[:, 2], rope[:, 0], rope[:, 1],
                                           ALU.add).then_inc(sig(4, "rope_sum"), 1)

                    def rope_low(t, p, a):
                        pool.wait_ge(sig(4, "qk_hi"), t * 2 + a + 1)
                        pool.tensor_tensor(qk_hl[p][:, a, 1], rope[:, 2], qk_hl[p][:, a, 0].bitcast(F32),
                                           ALU.subtract).then_inc(sig(4, "qk_hl"), 1)

                    def value_rest(t, p, i):
                        pool.wait_ge(sig(4, "v_part"), t * 2 + i + 1)
                        parts = v_parts[p][:, :, :, HD * i:HD * i + HD]
                        cur = v32 if i == 0 else vrest[:, 0]
                        pool.tensor_tensor(vrest[:, i].rearrange("p b (h d) -> p b h d", d=HD),
                                           cur[:].rearrange("p b (h d) -> p b h d", d=HD), parts,
                                           ALU.subtract).then_inc(sig(4, "v_rest"), 1)

                    def step4(t, p, h, more):
                        n, q = t + 1, 1 - p
                        if h == 1 and more:
                            rstd_of(4)(n, q)
                        if h == 3 and more:
                            bias(n)
                        if h in (6, 8) and more:
                            rope_sum(n, h // 8)
                        pool.wait_ge(sig(4, "prob"), t * 2 * HEADS + 2 * h + 2)
                        s, kb = h % HP, slice(BLK - POOL_KB, BLK)
                        pool.tensor_tensor(prob_lo[:, s, kb], prob[:, s, kb], prob_hi(s)[:, kb],
                                           ALU.subtract).then_inc(sig(4, "lo_pool"), 1)
                        if h == 4 and more:
                            x_low(n, q)
                        if h in (7, 8) and more:
                            rope_low(n, q, h - 7)
                        if h in (9, 12) and more:
                            value_rest(n, q, (h - 9) // 3)

                    def head4(t, p):
                        rstd_of(4)(t, p)
                        bias(t)
                        x_low(t, p)
                        for a in range(2):
                            rope_sum(t, a)
                            rope_low(t, p, a)
                        for i in range(2):
                            value_rest(t, p, i)
                        for h in range(EARLY):
                            step4(t, p, h, True)

                    def body4(t, p, more):
                        for h in range(EARLY, HEADS):
                            step4(t, p, h, more)
                        if more:
                            for h in range(EARLY):
                                step4(t + 1, 1 - p, h, two_more(t))

                    over_tiles(pool, 4, head4, body4)
                barrier(pool, ph + 1)

        @block.scalar
        def _(act):
            def copy(o, i):
                return act.activation(o, i, ACT.Copy)

            def transposed(ph, t, p):
                act.wait_ge(sig(ph, "tr"), t + 1)
                copy(xnT[:], wide(TR)).then_inc(sig(ph, "xnT"), 1)
                copy(xnT_hl[p][:, 0, :], wide(TR)).then_inc(sig(ph, "x_hi"), 1)

            def ffn0(ph):
                def hot(t, p):
                    act.wait_ge(sig(ph, "hotT"), t + 1)
                    src = wide(SM, dt=BF16)[0:3 * E0, 512:1024]
                    copy(onehotT[p][0:3 * E0, :], src).then_inc(sig(ph, "onehotT"), 1)

                def head(t, p):
                    transposed(ph, t, p)
                    if ph == 0:
                        act.wait_ge(setup, 2)
                    hot(t, p)

                def body(t, p, more):
                    for fb in range(FB0):
                        act.wait_ge(sig(ph, "h"), t * FB0 + fb + 1)
                        act.activation(g32[:, fb, :], wide(H0 + fb % 2), ACT.Gelu).then_inc(sig(ph, "gelu"), 1)
                        act.wait_ge(sig(ph, "gelu"), t * FB0 + fb + 1)
                        copy(g_hi[:, fb, :], g32[:, fb, :]).then_inc(sig(ph, "g_hi"), 1)
                        if fb == 1 and more:
                            transposed(ph, t + 1, 1 - p)
                    if more:
                        hot(t + 1, 1 - p)
                over_tiles(act, ph, head, body)

            def ffn1(ph):
                m = ffn1_mem

                def sigmoid(t, p):
                    act.wait_ge(sig(ph, "logit"), t + 1)
                    act.activation(m["sig"][:], m["logit"][:], ACT.Sigmoid).then_inc(sig(ph, "sigm"), 1)

                def gateT(t, p):
                    act.wait_ge(sig(ph, "gT"), t + 1)
                    copy(m["gateT"][p][0:3 * E1, :], wide(TR, dt=BF16)[0:3 * E1, 0:512])\
                        .then_inc(sig(ph, "gateT"), 1)

                def head(t, p):
                    transposed(ph, t, p)
                    sigmoid(t, p)
                    act.wait_ge(sig(ph, "zeroed"), 1 + FIRST[ph] // TILES)
                    gateT(t, p)

                def high(t, fb):
                    act.wait_ge(sig(ph, "m"), t * FB1 + fb + 1)
                    copy(m["hi"][:, fb % 4, :], m["m32"][:, fb % 4, :]).then_inc(sig(ph, "hi"), 1)

                def body(t, p, more):
                    for fb in range(FB1):
                        act.wait_ge(sig(ph, "h"), t * FB1 + fb + 1)
                        act.activation(m["relu"][:, fb % 4, :], wide(h1_banks[fb % 3]), ACT.Relu)\
                           .then_inc(sig(ph, "relu"), 1)
                        if fb >= 1:
                            high(t, fb - 1)
                        if more and fb == 3:
                            transposed(ph, t + 1, 1 - p)
                        if more and fb == 8:
                            sigmoid(t + 1, 1 - p)
                        if more and fb == 12:
                            gateT(t + 1, 1 - p)
                    high(t, FB1 - 1)
                    act.wait_ge(sig(ph, "y"), t + 1)
                    copy(m["yT"][:], wide(Y1)).then_inc(sig(ph, "yT"), 1)
                over_tiles(act, ph, head, body)

            def attention0():
                ph = 1

                def head(t, p):
                    transposed(ph, t, p)
                    act.wait_ge(sig(ph, "w"), t + 1)
                    copy(w32[p][:], wide(WT)).then_inc(sig(ph, "w32"), 1)
                    act.activation(wsq[p][:], wide(WT), ACT.Square, accum_out=norm2[:]).then_inc(sig(ph, "wsq"), 1)
                    act.wait_ge(sig(ph, "s_shift"), t + 1)
                    act.activation(sexp[:], sexp[:], ACT.Exp).then_inc(sig(ph, "s_exp"), 1)

                def second(t, p):
                    act.wait_ge(sig(ph, "piT"), t + 1)
                    copy(piT[:], wide(PT)).then_inc(sig(ph, "piT_sb"), 1)
                    act.wait_ge(sig(ph, "pi_rows"), t + 1)
                    act.activation(pi_rows[:], wide(PR), ACT.Copy, accum_out=pi_sum[:])\
                       .then_inc(sig(ph, "pi_sum"), 1)

                def body(t, p, more):
                    second(t, p)
                    if more:
                        head(t + 1, 1 - p)
                over_tiles(act, ph, head, body)

            def attention1():
                ph = 4
                one_row = small[:, 10:11]

                def queries(t, g, dst, name):
                    act.wait_ge(sig(ph, name), t * GROUPS + g + 1)
                    copy(dst, wide(MISC)).then_inc(sig(ph, name + "_sb"), 1)

                def key_pads(t, g):
                    act.wait_ge(sig(ph, "ks"), t * GROUPS + g + 1)
                    for j in range(HPG):
                        r = slice(32 * j, 32 * j + 32)
                        last = act.activation(k_pad[r, HPG * g + j, :], ps[r, MISC, :], ACT.Identity,
                                              bias=one_row[r])
                    last.then_inc(sig(ph, "k_pad"), 1)

                def head_a(t, p):
                    act.wait_ge(sig(ph, "tr"), t + 1)
                    copy(xnT[:], wide(MISC)).then_inc(sig(ph, "xnT"), 1)
                    copy(xnT_hl[p][:, 0, :], wide(MISC)).then_inc(sig(ph, "x_hi"), 1)

                def head_b(t, p):
                    act.wait_ge(sig(ph, "v"), t + 1)
                    copy(v32[:], rows4(MISC)).then_inc(sig(ph, "v32"), 1)
                    part(t, p, 0)

                def part(t, p, i):
                    if i > 0:
                        act.wait_ge(sig(ph, "v_rest"), 2 * t + i)
                    else:
                        act.wait_ge(sig(ph, "v32"), t + 1)
                    src = v32 if i == 0 else vrest[:, i - 1]
                    copy(v_parts[p][:, :, :, HD * i:HD * i + HD], src[:].rearrange("p b (h d) -> p b h d", d=HD))\
                        .then_inc(sig(ph, "v_part" if i < 2 else "v_parts"), 1)

                def rope_high(t, p, a):
                    act.wait_ge(sig(ph, "rope_sum"), t * 2 + a + 1)
                    copy(qk_hl[p][:, a, 0], rope[:, 2]).then_inc(sig(ph, "qk_hi"), 1)

                def exps(t, h):
                    s = h % HP
                    for half in range(2):
                        act.wait_ge(sig(ph, "st"), t * 2 * HEADS + 2 * h + half + 1)
                        b0 = PASS2 + 2 * half
                        act.activation(prob[:, s, 2 * half:2 * half + 2, :], ps[:, b0:b0 + 2, :], ACT.Exp,
                                       scale=SCALE).then_inc(sig(ph, "prob"), 1)

                def project(t):
                    act.wait_ge(sig(ph, "oT"), t + 1)
                    copy(oT[:], wide(MISC)).then_inc(sig(ph, "oT_sb"), 1)

                def step(t, p, h, more, before=None):
                    n, q = t + 1, 1 - p
                    exps(t, h)
                    if h == 0:
                        key_pads(t, 2)
                    if h == 1:
                        queries(t, 2, q_st[:, 0, :], "qs")
                        if before is not None:
                            project(before)
                    if h == 3:
                        queries(t, 1, q_sh[:, 1, :], "qsh")
                    if h == 3 and more:
                        head_a(n, q)
                    if h == 4:
                        key_pads(t, 3)
                    if h == 5:
                        queries(t, 3, q_st[:, 1, :], "qs")
                    if h == 7:
                        queries(t, 2, q_sh[:, 0, :], "qsh")
                    if h in (7, 8) and more:
                        rope_high(n, q, h - 7)
                    if h == 8 and more:
                        head_b(n, q)
                    if h == 9 and more:
                        key_pads(n, 0)
                    if h == 10 and more:
                        queries(n, 0, q_st[:, 0, :], "qs")
                    if h == 11:
                        queries(t, 3, q_sh[:, 1, :], "qsh")
                        if more:
                            part(n, q, 1)
                    if h == 12 and more:
                        key_pads(n, 1)
                    if h == 13 and more:
                        queries(n, 1, q_st[:, 1, :], "qs")
                    if h == 14 and more:
                        part(n, q, 2)
                    if h == 15 and more:
                        queries(n, 0, q_sh[:, 0, :], "qsh")

                def head(t, p):
                    head_a(t, p)
                    head_b(t, p)
                    for a in range(2):
                        rope_high(t, p, a)
                    for i in (1, 2):
                        part(t, p, i)
                    act.wait_ge(sig(ph, "zeroed"), 1)
                    key_pads(t, 0)
                    queries(t, 0, q_st[:, 0, :], "qs")
                    key_pads(t, 1)
                    queries(t, 1, q_st[:, 1, :], "qs")
                    queries(t, 0, q_sh[:, 0, :], "qsh")
                    for h in range(EARLY):
                        step(t, p, h, True)

                def body(t, p, more):
                    for h in range(EARLY, HEADS):
                        step(t, p, h, more)
                    if more:
                        for h in range(EARLY):
                            step(t + 1, 1 - p, h, two_more(t), before=t)
                    else:
                        project(t)
                over_tiles(act, ph, head, body)

            ffn0(0)
            barrier(act, 1)
            attention0()
            barrier(act, 2)
            ffn0(2)
            barrier(act, 3)
            ffn1(3)
            barrier(act, 4)
            attention1()
            barrier(act, 5)
            ffn1(5)
            barrier(act, 6)

        @block.vector
        def _(dve):
            def copy(o, i):
                return dve.tensor_copy(o, i)

            def sub(o, a, b):
                return dve.tensor_tensor(o, a, b, ALU.subtract)

            once = Chain(dve, sem("dve_once"), 0)

            def unstage(n, pieces):
                cols = (staged + list(views["staged_late"]))[n][1]
                src = (stage[n % 2] if n < len(staged) else stage_l[n - len(staged)])[:, 0:cols]
                dve.wait_ge(w_in, 16 * (n + 1))
                last = once.step(copy(pieces[0], src))
                if len(pieces) == 2:
                    once.settle()
                    last = once.step(sub(pieces[1], src, pieces[0].bitcast(F32)))
                once.settle()
                dve.sem_inc(stage_free, 1)

            def flat(ap):
                dims = "abcd"[:len(ap.shape) - 1]
                return ap if len(ap.shape) == 2 else ap.rearrange(f"p {' '.join(dims)} -> p ({' '.join(dims)})")

            def x_block(ph, t, b):
                return x[:, bass.ds((t - FIRST[ph]) * BLK + b, 1), :]

            def x_tile(ph, t):
                return x[:, bass.ds((t - FIRST[ph]) * BLK, BLK), :]

            def normalise(ph, t, part):
                if part == 0:
                    if ph > 0:
                        dve.wait_ge(sig(ph - 1, "x_done"), (t - FIRST[ph] + FIRST[ph - 1]) * 4 + 4)
                    for b in range(BLK):
                        last = dve.bn_stats(stats[:, b, :], x_block(ph, t, b))
                    last.then_inc(sig(ph, "stats"), 1)
                    pass_wait(dve, sig(ph, "stats"), t + 1)
                    for b in range(BLK):
                        last = dve.bn_aggr(meanvar[:, b, :], stats[:, b, :])
                    last.then_inc(sig(ph, "meanvar"), 1)
                else:
                    dve.wait_ge(sig(ph, "rstd"), t + 1)
                    for b in range(BLK):
                        last = dve.tensor_scalar(xn[:, b, :], x_block(ph, t, b),
                                                 meanvar[:, b, 0:1], rstd[:, b:b + 1],
                                                 ALU.subtract, ALU.mult)
                    last.then_inc(sig(ph, "xn"), 1)

            def x_low(ph, t, p):
                dve.wait_ge(sig(ph, "x_hi"), t + 1)
                sub(xnT_hl[p][:, 1, :], xnT[:], xnT_hl[p][:, 0, :].bitcast(F32)).then_inc(sig(ph, "x_lo"), 1)


            dve.wait_ge(consts, 16 * 16)
            dve.wait_ge(setup, 2)
            resid = bias_f[:]
            for part in range(3):
                once.step(copy(bias_p[:, part], resid))
                once.settle()
                if part < 2:
                    once.step(sub(bias_r[:, part], resid, bias_p[:, part]))
                    once.settle()
                    resid = bias_r[:, part]
            for k in range(2):
                once.step(dve.tensor_scalar(bias_r[:, 0, k], bias_p[:, 0, k], small[:, 3 * k:3 * k + 1], None,
                                            ALU.mult))
                once.settle()
                once.step(dve.scalar_tensor_tensor(out=bias_r[:, 1, k], in0=bias_p[:, 1, k],
                                                   scalar=small[:, 3 * k + 1:3 * k + 2],
                                                   in1=bias_r[:, 0, k], op0=ALU.mult, op1=ALU.add))
                once.settle()
                once.step(dve.scalar_tensor_tensor(out=bias_m[:, k], in0=bias_p[:, 2, k],
                                                   scalar=small[:, 3 * k + 2:3 * k + 3],
                                                   in1=bias_r[:, 1, k], op0=ALU.mult, op1=ALU.add))
            once.step(dve.tensor_scalar(ones3[:], ones3[:], small[:, 11:12], None, ALU.add))
            once.step(dve.tensor_tensor(temp_ind[:], temp_b[:], small[:, 16:16 + HEADS], ALU.mult))
            unstage(0, (flat(sel_expert[:]),))
            unstage(1, (flat(w1_hl[:, 0]), flat(w1_hl[:, 1])))
            unstage(2, (flat(w2_hl[:, 0]), flat(w2_hl[:, 1])))
            once.step(copy(ident_b[:], ident[:]))
            once.step(copy(qkvT_hl[:, 0], qkv_f[:, 0]))
            once.settle()
            once.step(sub(qkvT_hl[:, 1], qkv_f[:, 0], qkvT_hl[:, 0].bitcast(F32)))
            once.settle()
            dve.sem_inc(setup, 1)

            def ffn0(ph):
                rc = Chain(dve, sig(ph, "route_steps"), 8)
                ac = Chain(dve, sig(ph, "add_steps"), BLK * E0)

                def route(t, p):
                    rc.tile(t)
                    dve.wait_ge(sig(ph, "lg"), t + 1)
                    lg = ps[:, SM, 0:BLK * E0].rearrange("p (b e) -> p b e", e=E0)
                    bc = [P, BLK, E0]
                    rc.step(dve.tensor_tensor(logit[:], lg, gate_b[:].unsqueeze(1).broadcast_to(bc), ALU.add))
                    rc.settle()
                    rc.step(dve.tensor_reduce(best[:], logit[:], AXX, ALU.max))
                    rc.settle()
                    rc.step(dve.tensor_tensor(equal[:], logit[:], best[:].unsqueeze(2).broadcast_to(bc),
                                              ALU.is_equal))
                    rc.settle()
                    rc.step(dve.tensor_tensor(equal[:], equal[:], small[:, 6:10].unsqueeze(1).broadcast_to(bc),
                                              ALU.mult))
                    rc.settle()
                    rc.step(dve.tensor_reduce(first[:], equal[:], AXX, ALU.max))
                    rc.settle()
                    rc.step(dve.tensor_tensor(logit[:], equal[:], first[:].unsqueeze(2).broadcast_to(bc),
                                              ALU.is_equal))
                    rc.settle()
                    rc.step(dve.tensor_scalar(half_hot[p][:], logit[:], 0.5, None, ALU.mult))
                    for k in range(3):
                        last = copy(onehot[:, :, E0 * k:E0 * k + E0], logit[:])
                    rc.step(last)
                    rc.settle()
                    dve.sem_inc(sig(ph, "hot"), 1)

                def masked(t, p, e):
                    dve.wait_ge(sig(ph, "mask"), t * E0 + e + 1)
                    dve.tensor_tensor(x_masked[p][:, e], xnT_hl[p][:].bitcast(F32),
                                      wide(MASK + e % 2).unsqueeze(1).broadcast_to([P, 2, SEQ]),
                                      ALU.mult).then_inc(sig(ph, "x_masked"), 1)

                def g_low(t, fb):
                    dve.wait_ge(sig(ph, "g_hi"), t * FB0 + fb + 1)
                    sub(g_lo[:, fb], g32[:, fb], g_hi[:, fb].bitcast(F32)).then_inc(sig(ph, "g_lo"), 1)

                def add_y(t, p, tb):
                    dve.wait_ge(sig(ph, "y"), t * BLK + tb + 1)
                    xt = x_block(ph, t, tb)
                    for e in range(E0):
                        last = dve.scalar_tensor_tensor(
                            out=xt, in0=ps[:, Y0 + tb % 2, e * D:e * D + D].unsqueeze(1),
                            scalar=half_hot[p][:, tb, e:e + 1],
                            in1=xt, op0=ALU.mult, op1=ALU.add)
                        ac.step(last)
                        ac.settle()
                    dve.sem_inc(sig(ph, "x_done"), 1)

                def head(t, p):
                    if ph == 0:
                        dve.wait_ge(x_first, 16)
                    normalise(ph, t, 0)
                    normalise(ph, t, 1)
                    x_low(ph, t, p)
                    route(t, p)
                    for e in range(E0):
                        masked(t, p, e)

                def body(t, p, more):
                    n, q = t + 1, 1 - p
                    ac.tile(t)
                    if more:
                        if ph == 0 and p == 1:
                            dve.wait_ge(x_rest, 16)
                        normalise(ph, n, 0)
                        normalise(ph, n, 1)
                    g_low(t, 0)
                    g_low(t, 1)
                    if more:
                        x_low(ph, n, q)
                    g_low(t, 2)
                    g_low(t, 3)
                    if more:
                        route(n, q)
                    for tb in range(BLK):
                        add_y(t, p, tb)
                        if more and tb in (0, 1):
                            masked(n, q, 2 * tb)
                            masked(n, q, 2 * tb + 1)
                over_tiles(dve, ph, head, body)

            def ffn1(ph):
                m = ffn1_mem
                rc = Chain(dve, sig(ph, "route_steps"), 11)

                def top(t, p):
                    rc.tile(t)
                    dve.wait_ge(sig(ph, "lg"), t + 1)
                    rc.step(copy(m["logit"][:], rows4(SM)[:, :, 0:E1]))
                    rc.settle()
                    dve.sem_inc(sig(ph, "logit"), 1)
                    for b in range(BLK):
                        last = dve.max(m["top8"][:, b], m["logit"][:, b])
                    rc.step(last)
                    rc.settle()
                    rc.step(dve.memset(m["top8"][:, :, TOP1:8], BIG))
                    rc.settle_alone()
                    for b in range(BLK):
                        last = dve.match_replace(m["taken"][:, b], m["top8"][:, b], m["logit"][:, b], -BIG)
                    rc.step(last)
                    rc.settle()
                    rc.step(dve.tensor_tensor(m["gate"][:], m["taken"][:], m["logit"][:], ALU.is_lt))
                    rc.settle()
                    dve.wait_ge(sig(ph, "sigm"), t + 1)
                    rc.step(dve.tensor_tensor(m["gate"][:], m["gate"][:], m["sig"][:], ALU.mult))
                    rc.settle()
                    cur = m["gate"][:]
                    for part in range(3):
                        to = m["parts"][:, :, E1 * part:E1 * part + E1]
                        rc.step(copy(to, cur))
                        rc.settle()
                        if part < 2:
                            rc.step(sub(m["rest"][:, part], cur, to))
                            rc.settle()
                            cur = m["rest"][:, part]
                    dve.sem_inc(sig(ph, "gates"), 1)

                def low(t, fb):
                    if fb not in POOL_FB:
                        dve.wait_ge(sig(ph, "hi"), t * FB1 + fb + 1)
                        sub(m["lo"][:, fb % 4], m["m32"][:, fb % 4], m["hi"][:, fb % 4].bitcast(F32))\
                            .then_inc(sig(ph, "lo_dve"), 1)

                def head(t, p):
                    normalise(ph, t, 0)
                    normalise(ph, t, 1)
                    x_low(ph, t, p)
                    top(t, p)

                def body(t, p, more):
                    n, q = t + 1, 1 - p
                    for fb in range(FB1):
                        dve.wait_ge(sig(ph, "relu"), t * FB1 + fb + 1)
                        dve.tensor_tensor(m["m32"][:, fb % 4], m["relu"][:, fb % 4], wide(G1 + fb % 2),
                                          ALU.mult).then_inc(sig(ph, "m"), 1)
                        if fb >= 1:
                            low(t, fb - 1)
                        if more and fb == 0:
                            normalise(ph, n, 0)
                        if more and fb == 2:
                            normalise(ph, n, 1)
                        if more and fb == 5:
                            x_low(ph, n, q)
                        if more and fb == 8:
                            top(n, q)
                    low(t, FB1 - 1)
                    dve.wait_ge(sig(ph, "y_rows"), t + 1)
                    dve.scalar_tensor_tensor(out=x_tile(ph, t), in0=rows4(TR), scalar=0.5, in1=x_tile(ph, t),
                                             op0=ALU.mult, op1=ALU.add).then_inc(sig(ph, "x_done"), 4)
                over_tiles(dve, ph, head, body)

            def attention0():
                ph = 1
                hc = Chain(dve, sig(ph, "head_steps"), 7)
                bc_ = Chain(dve, sig(ph, "body_steps"), 8)

                def head(t, p):
                    normalise(ph, t, 0)
                    normalise(ph, t, 1)
                    x_low(ph, t, p)
                    hc.tile(t)
                    dve.wait_ge(sig(ph, "wsq"), t + 1)
                    hc.step(dve.tensor_scalar(inv2[:], norm2[:], 1e-24, None, ALU.max))
                    hc.settle()
                    hc.step(dve.reciprocal(inv2[:], inv2[:]))
                    hc.settle()
                    hc.step(dve.tensor_scalar(norm_ind[:], temp_ind[:], inv2[:], None, ALU.mult))
                    hc.settle()
                    dve.sem_inc(sig(ph, "norm_ind"), 1)
                    dve.wait_ge(sig(ph, "s"), t + 1)
                    s = ps[:, SC, 0:BLK * HEADS].rearrange("p (b h) -> p b h", h=HEADS)
                    bc = [P, BLK, HEADS]
                    hc.step(dve.tensor_reduce(smax[:], s, AXX, ALU.max))
                    hc.settle()
                    dve.tensor_tensor(sexp[:], s, smax[:].unsqueeze(2).broadcast_to(bc), ALU.subtract)\
                       .then_inc(sig(ph, "s_shift"), 1)
                    dve.wait_ge(sig(ph, "s_exp"), t + 1)
                    hc.step(dve.tensor_reduce(ssum[:], sexp[:], AXX, ALU.add))
                    hc.settle()
                    hc.step(dve.reciprocal(ssum[:], ssum[:]))
                    hc.settle()
                    hc.step(dve.tensor_tensor(pi[p][:, :, 0:HEADS], sexp[:],
                                              ssum[:].unsqueeze(2).broadcast_to(bc), ALU.mult))
                    hc.settle()
                    dve.sem_inc(sig(ph, "pi"), 1)

                def body(t, p, more):
                    bc_.tile(t)
                    dve.wait_ge(sig(ph, "pi_sum"), t + 1)
                    bc_.step(dve.tensor_tensor_reduce(out=prod[:], in0=wsq[p][:], in1=pi_rows[:], scale=1.0,
                                                      scalar=0.0, op0=ALU.mult, op1=ALU.add,
                                                      accum_out=dots[:, 0:1]))
                    bc_.step(dve.tensor_scalar(dots[:, 1:2], pi_sum[:], 1e-8, None, ALU.add))
                    bc_.settle()
                    bc_.step(dve.reciprocal(dots[:, 2:3], dots[:, 1:2]))
                    bc_.settle()
                    bc_.step(dve.tensor_scalar(dots[:, 3:4], dots[:, 0:1], dots[:, 2:3], 1.0,
                                               ALU.mult, ALU.add))
                    bc_.settle()
                    bc_.step(dve.reciprocal(dots[:, 0:1], dots[:, 3:4]))
                    bc_.settle()
                    bc_.step(dve.tensor_scalar(dots[:, 1:2], dots[:, 0:1], -1.0, None, ALU.mult))
                    bc_.settle()
                    dve.scalar_tensor_tensor(out=outT[:], in0=w32[p][:], scalar=dots[:, 1:2], in1=pi_rows[:],
                                             op0=ALU.mult, op1=ALU.mult).then_inc(sig(ph, "outT"), 1)
                    if more:
                        head(t + 1, 1 - p)
                    dve.wait_ge(sig(ph, "y"), t + 1)
                    bc_.step(dve.tensor_tensor(x_tile(ph, t), x_tile(ph, t), rows4(YA), ALU.add))
                    bc_.settle()
                    bc_.step(dve.tensor_tensor(x_tile(ph, t), x_tile(ph, t),
                                               out_b0[:].unsqueeze(1).broadcast_to([P, BLK, D]), ALU.add))
                    bc_.settle()
                    dve.sem_inc(sig(ph, "x_done"), 4)
                over_tiles(dve, ph, head, body)

            def attention1():
                ph = 4

                def rotary(t, i):
                    dve.wait_ge(sig(ph, "qk"), t * 4 + i + 1)
                    if i == 2:
                        dve.wait_ge(sig(ph, "rope_sum"), t * 2 + 1)
                    dve.tensor_tensor(rope[:, i % 2], wide(MISC), (cos_t, sin_t)[i % 2][:],
                                      ALU.mult).then_inc(sig(ph, "qk_read"), 1)

                def maxima(t, g, j, blocks=range(BLK)):
                    for b in blocks:
                        dve.wait_ge(sig(ph, "s1"), (t * GROUPS + g) * 16 + 4 * j + b + 1)
                        dve.tensor_reduce(qmax[:, g % 2, j, b:b + 1], wide(PASS1 + b % 2), AXX,
                                          ALU.max).then_inc(sig(ph, "qmax"), 1)

                def minus_max(t, g):
                    dve.wait_ge(sig(ph, "qmax"), (t * GROUPS + g + 1) * 16)
                    to = shift[:, g % 2].rearrange("p b (j r) -> p b j r", r=32)[:, :, :, 3 * HD]
                    dve.tensor_scalar(to, qmax[:, g % 2].rearrange("p j b -> p b j"), -1.0, None,
                                      ALU.mult).then_inc(sig(ph, "shift"), 1)

                def low(t, h):
                    dve.wait_ge(sig(ph, "prob"), t * 2 * HEADS + 2 * h + 1)
                    s, kb = h % HP, slice(0, BLK - POOL_KB)
                    sub(prob_lo[:, s, kb], prob[:, s, kb], prob_hi(s)[:, kb]).then_inc(sig(ph, "lo_dve"), 1)

                def output(t, g):
                    dve.wait_ge(sig(ph, "pv"), (t * GROUPS + g + 1) * HPG)
                    o = ps[:, OB, 0:HPG * BLK * VC].rearrange("p (n c) -> p n c", c=VC)
                    dve.tensor_reduce(o_sum[:], o[:, :, 0:3 * HD].rearrange("p n (k d) -> p n d k", k=3),
                                      AXX, ALU.add)
                    dve.reciprocal(o_rcp[:], o[:, :, 3 * HD]).then_inc(sig(ph, "o_read"), 1)
                    dve.wait_ge(sig(ph, "o_read"), t * GROUPS + g + 1)
                    to = o_all[:].rearrange("p b (h d) -> p h b d", d=HD)[:, HPG * g:HPG * g + HPG]
                    src = o_sum[:].rearrange("p (j b) d -> p j b d", j=HPG)
                    rcp = o_rcp[:].rearrange("p (j b) -> p j b", j=HPG)
                    last = dve.tensor_tensor(to, src, rcp.unsqueeze(3).broadcast_to([P, HPG, BLK, HD]), ALU.mult)
                    if g == GROUPS - 1:
                        last.then_inc(sig(ph, "o_all"), 1)

                def head(t, p):
                    normalise(ph, t, 0)
                    normalise(ph, t, 1)
                    for i in range(4):
                        rotary(t, i)
                    for h in range(AHEAD):
                        maxima(t, h // HPG, h % HPG)
                        if h == HPG - 1:
                            minus_max(t, 0)
                    for h in range(EARLY):
                        step(t, p, h, True)

                def add_projected(t):
                    dve.wait_ge(sig(ph, "y"), t + 1)
                    dve.wait_ge(sig(ph, "biased"), t + 1)
                    dve.tensor_tensor(x_tile(ph, t), x_tile(ph, t), rows4(MISC), ALU.add)\
                       .then_inc(sig(ph, "x_done"), 4)

                def step(t, p, h, more, before=None):
                    n = t + 1
                    if h == 1 and more:
                        normalise(ph, n, 0)
                    if h == 2 and more:
                        normalise(ph, n, 1)
                    if h in (6, 7, 8) and more:
                        rotary(n, {6: 0, 7: 2, 8: 3}[h])
                    ahead = h + AHEAD
                    if ahead < HEADS or more:
                        maxima(t + ahead // HEADS, ahead % HEADS // HPG, ahead % HPG, (0, 1))
                    if h >= 1:
                        low(t, h - 1)
                    elif before is not None:
                        low(before, HEADS - 1)
                    if h == 6 and more:
                        rotary(n, 1)
                    if ahead < HEADS or more:
                        maxima(t + ahead // HEADS, ahead % HEADS // HPG, ahead % HPG, (2, 3))
                    if h % HPG == 0 and h > 0:
                        output(t, h // HPG - 1)
                    if h == 0 and before is not None:
                        output(before, GROUPS - 1)
                    if h == 2 and before is not None:
                        add_projected(before)
                    if ahead % HPG == HPG - 1 and (ahead < HEADS or more):
                        minus_max(t + ahead // HEADS, ahead % HEADS // HPG)

                def body(t, p, more):
                    for h in range(EARLY, HEADS):
                        step(t, p, h, more)
                    if more:
                        for h in range(EARLY):
                            step(t + 1, 1 - p, h, two_more(t), before=t)
                    else:
                        low(t, HEADS - 1)
                        output(t, GROUPS - 1)
                        add_projected(t)
                over_tiles(dve, ph, head, body)

            ffn0(0)
            unstage(3, (flat(sel_gate[:]),))
            unstage(4, (keys_hl[:, 0], keys_hl[:, 1]))
            unstage(5, (flat(vals_hl[:, 0]), flat(vals_hl[:, 1])))
            barrier(dve, 1)
            dve.wait_ge(sig(1, "zeroed"), 1)
            attention0()
            barrier(dve, 2)
            ffn0(2)
            barrier(dve, 3)
            ffn1(3)
            barrier(dve, 4)
            dve.wait_ge(sig(4, "tables"), 16 * 5)
            unstage(6, (flat(stack_sel[:]),))
            qk_stage = stage_l[1][:, 0:4 * P].rearrange("p (a b) -> p a b", a=4)
            dve.wait_ge(w_in, 16 * 8)
            once.step(copy(w_qk[:, :, 0], qk_stage))
            once.settle()
            once.step(sub(w_qk[:, :, 1], qk_stage, w_qk[:, :, 0].bitcast(F32)))
            once.step(copy(ident_r[:], ident[:]))
            once.settle()
            dve.sem_inc(sig(4, "weights"), 1)
            attention1()
            barrier(dve, 5)
            ffn1(5)
            barrier(dve, 6)

        @block.tensor
        def _(pe):
            def three(dst, w_hi, w_lo, x_hi, x_lo, start=True, stop=True):
                pe.matmul(dst, w_hi, x_hi, start=start, stop=False)
                pe.matmul(dst, w_hi, x_lo, start=False, stop=False)
                return pe.matmul(dst, w_lo, x_hi, start=False, stop=stop)

            def transpose_in(ph, t, bank):
                pe.wait_ge(sig(ph, "xn"), t + 1)
                for b in range(BLK):
                    last = pe.transpose(rows4(bank)[:, b], xn[:, b], ident[:])
                last.then_inc(sig(ph, "tr"), 1)

            def route(ph, t, weights, n):
                pe.wait_ge(sig(ph, "xnT"), t + 1)
                for b in range(BLK):
                    dst = ps[:, SM, b * E0:b * E0 + E0] if n == E0 else rows4(SM)[:, b, 0:n]
                    last = pe.matmul(dst, xnT[:, b * P:b * P + P], weights, start=True, stop=True)
                last.then_inc(sig(ph, "lg"), 1)

            def ffn0(ph):
                def hotT(t):
                    pe.wait_ge(sig(ph, "hot"), t + 1)
                    dst = wide(SM, dt=BF16)[0:3 * E0, 512:1024]
                    for b in range(BLK):
                        last = pe.transpose(dst[:, b * P:b * P + P], onehot[:, b], ident_b[:])
                    last.then_inc(sig(ph, "hotT"), 1)

                def mask(t, p, e):
                    if e == 0:
                        pe.wait_ge(sig(ph, "onehotT"), t + 1)
                    if e >= 2:
                        pe.wait_ge(sig(ph, "x_masked"), t * E0 + e - 1)
                    pe.matmul(wide(MASK + e % 2), sel_expert[:, e], onehotT[p][:], start=True, stop=True)\
                      .then_inc(sig(ph, "mask"), 1)

                def up(t, p, fb):
                    dst = wide(H0 + fb % 2)
                    if fb >= 2:
                        pe.wait_ge(sig(ph, "gelu"), t * FB0 + fb - 1)
                    pe.matmul(dst, bias_m[:, 0, fb * P:fb * P + P], onehotT[p][:], start=True, stop=False)
                    for e in range(E0):
                        if fb == 0:
                            pe.wait_ge(sig(ph, "x_masked"), t * E0 + e + 1)
                        c = slice(fb * P, fb * P + P)
                        last = three(dst, w1_hl[:, 0, e, c], w1_hl[:, 1, e, c], x_masked[p][:, e, 0],
                                     x_masked[p][:, e, 1], start=False, stop=(e == E0 - 1))
                    last.then_inc(sig(ph, "h"), 1)

                def down(t, tb):
                    dst = wide(Y0 + tb % 2)
                    if tb >= 2:
                        pe.wait_ge(sig(ph, "x_done"), t * BLK + tb - 1)
                    if tb == 0:
                        pe.wait_ge(sig(ph, "g_lo"), t * FB0 + 1)
                    pe.matmul(dst, ones3[:], bias_m[:, 1], start=True, stop=False)
                    c = slice(tb * P, tb * P + P)
                    for fb in range(FB0):
                        if tb == 0 and fb > 0:
                            pe.wait_ge(sig(ph, "g_lo"), t * FB0 + fb + 1)
                        pe.matmul(dst, g_hi[:, fb, c], w2_hl[:, 0, fb], start=False, stop=False)
                        pe.matmul(dst, g_hi[:, fb, c], w2_hl[:, 1, fb], start=False, stop=False)
                        last = pe.matmul(dst, g_lo[:, fb, c], w2_hl[:, 0, fb], start=False,
                                         stop=(fb == FB0 - 1))
                    last.then_inc(sig(ph, "y"), 1)

                def head(t, p):
                    transpose_in(ph, t, TR)
                    route(ph, t, gate_w[:], E0)
                    hotT(t)
                    for e in range(E0):
                        mask(t, p, e)

                def body(t, p, more):
                    n, q = t + 1, 1 - p
                    for fb in range(FB0):
                        up(t, p, fb)
                        if more and fb == 1:
                            transpose_in(ph, n, TR)
                        if more and fb == 3:
                            route(ph, n, gate_w[:], E0)
                    for tb in range(BLK):
                        down(t, tb)
                        if more and tb == 0:
                            hotT(n)
                            mask(n, q, 0)
                            mask(n, q, 1)
                        if more and tb == 1:
                            mask(n, q, 2)
                            mask(n, q, 3)
                over_tiles(pe, ph, head, body)

            def ffn1(ph):
                m = ffn1_mem

                def gateT(t, p):
                    pe.wait_ge(sig(ph, "gates"), t + 1)
                    for b in range(BLK):
                        last = pe.transpose(wide(TR, dt=BF16)[0:3 * E1, b * P:b * P + P], m["parts"][:, b],
                                            ident_b[:])
                    last.then_inc(sig(ph, "gT"), 1)

                def up(t, p, fb):
                    if fb >= 3:
                        pe.wait_ge(sig(ph, "relu"), t * FB1 + fb - 2)
                    c = slice(fb * P, fb * P + P)
                    three(wide(h1_banks[fb % 3]), keys_hl[:, 0, c], keys_hl[:, 1, c], xnT_hl[p][:, 0],
                          xnT_hl[p][:, 1])
                    if fb >= 2:
                        pe.wait_ge(sig(ph, "m"), t * FB1 + fb - 1)
                    pe.matmul(wide(G1 + fb % 2), sel_gate[:, fb], m["gateT"][p][:], start=True, stop=True)\
                      .then_inc(sig(ph, "h"), 1)

                def down(t, fb):
                    k = sum(f in POOL_FB for f in range(fb + 1))
                    if fb in POOL_FB:
                        pe.wait_ge(sig(ph, "lo_pool"), t * len(POOL_FB) + k)
                    else:
                        pe.wait_ge(sig(ph, "lo_dve"), t * (FB1 - len(POOL_FB)) + fb + 1 - k)
                    s = fb % 4
                    last = three(wide(Y1), vals_hl[:, 0, fb], vals_hl[:, 1, fb], m["hi"][:, s], m["lo"][:, s],
                                 start=(fb == 0), stop=(fb == FB1 - 1))
                    if fb == FB1 - 1:
                        last.then_inc(sig(ph, "y"), 1)

                def start(t, p):
                    pe.wait_ge(sig(ph, "x_lo"), t + 1)
                    pe.wait_ge(sig(ph, "gateT"), t + 1)

                def head(t, p):
                    transpose_in(ph, t, TR)
                    route(ph, t, router1[:], E1)
                    gateT(t, p)
                    start(t, p)

                def body(t, p, more):
                    n, q = t + 1, 1 - p
                    if not (isinstance(t, int) and t == FIRST[ph]):
                        start(t, p)
                    for fb in range(FB1 + LEAD):
                        if fb < FB1:
                            up(t, p, fb)
                        if fb >= LEAD:
                            down(t, fb - LEAD)
                        if more and fb == 4:
                            transpose_in(ph, n, TR)
                        if more and fb == 6:
                            route(ph, n, router1[:], E1)
                        if more and fb == 12:
                            gateT(n, q)
                    pe.wait_ge(sig(ph, "yT"), t + 1)
                    if more:
                        pe.wait_ge(sig(ph, "gateT"), n + 1)
                    for b in range(BLK):
                        last = pe.transpose(rows4(TR)[:, b], m["yT"][:, b * P:b * P + P], ident[:])
                    last.then_inc(sig(ph, "y_rows"), 1)
                over_tiles(pe, ph, head, body)

            def attention0():
                ph = 1

                def head(t, p):
                    transpose_in(ph, t, TR)
                    pe.wait_ge(sig(ph, "x_lo"), t + 1)
                    three(wide(WT), qkvT_hl[:, 0], qkvT_hl[:, 1], xnT_hl[p][:, 0], xnT_hl[p][:, 1])\
                        .then_inc(sig(ph, "w"), 1)
                    pe.wait_ge(sig(ph, "norm_ind"), t + 1)
                    for b in range(BLK):
                        last = pe.matmul(ps[:, SC, b * HEADS:b * HEADS + HEADS], wsq[p][:, b * P:b * P + P],
                                         norm_ind[:], start=True, stop=True)
                    last.then_inc(sig(ph, "s"), 1)

                def body(t, p, more):
                    pe.wait_ge(sig(ph, "pi"), t + 1)
                    for b in range(BLK):
                        last = pe.transpose(rows4(PT)[:, b], pi[p][:, b], ident[:])
                    last.then_inc(sig(ph, "piT"), 1)
                    pe.wait_ge(sig(ph, "piT_sb"), t + 1)
                    pe.matmul(wide(PR), head_rows[:], piT[:], start=True, stop=True)\
                      .then_inc(sig(ph, "pi_rows"), 1)
                    if more:
                        head(t + 1, 1 - p)
                    pe.wait_ge(sig(ph, "outT"), t + 1)
                    for b in range(BLK):
                        last = pe.matmul(rows4(YA)[:, b], outT[:, b * P:b * P + P], qkv_f[:, 1],
                                         start=True, stop=True)
                    last.then_inc(sig(ph, "y"), 1)
                over_tiles(pe, ph, head, body)

            def attention1():
                ph = 4

                def queries(t, g, p, name):
                    s = stack_sel[:, g]
                    if g == 0:
                        pe.wait_ge(sig(ph, "qk_hl"), 2 * t + 2)
                    pe.matmul(wide(MISC), s[:, 0], qk_hl[p][:, 1, 0], start=True, stop=False)
                    last = pe.matmul(wide(MISC), s[:, 1], qk_hl[p][:, 1, 1], start=False, stop=True)
                    if name == "qsh":
                        for b in range(BLK):
                            last = pe.matmul(rows4(MISC)[:, b], shift[:, g % 2, b], ident_r[:], start=False,
                                             stop=True, skip_group_check=True)
                    last.then_inc(sig(ph, name), 1)

                def keys(t, g, p):
                    s = stack_sel[:, g]
                    if g == 0:
                        pe.wait_ge(sig(ph, "qk_hl"), 2 * t + 1)
                    pe.matmul(wide(MISC), s[:, 2], qk_hl[p][:, 0, 0], start=True, stop=False)
                    pe.matmul(wide(MISC), s[:, 3], qk_hl[p][:, 0, 1], start=False, stop=True)\
                      .then_inc(sig(ph, "ks"), 1)
                def pass1(t, g, j, blocks=range(BLK)):
                    if j == 0 and 0 in blocks:
                        pe.wait_ge(sig(ph, "qs_sb"), t * GROUPS + g + 1)
                    for b in blocks:
                        if not (isinstance(t, int) and t == g == 0 and 4 * j + b < 2):
                            pe.wait_ge(sig(ph, "qmax"), (t * GROUPS + g) * 16 + 4 * j + b - 1)
                        pe.matmul(wide(PASS1 + b % 2), q_st[:, g % 2, b * P:b * P + P], k_pad[:, HPG * g + j],
                                  start=True, stop=True).then_inc(sig(ph, "s1"), 1)

                def pass2(t, h, half, first=False):
                    if h % HPG == 0 and half == 0:
                        pe.wait_ge(sig(ph, "qsh_sb"), t * GROUPS + h // HPG + 1)
                    for b in (2 * half, 2 * half + 1):
                        if b % 2 == 0 and not first:
                            pe.wait_ge(sig(ph, "prob"), t * 2 * HEADS + 2 * h - 1 + b // 2)
                        last = pe.matmul(wide(PASS2 + b), k_pad[:, h, b * P:b * P + P],
                                         q_sh[:, (h // HPG) % 2], start=True, stop=True)
                        if b % 2:
                            last.then_inc(sig(ph, "st"), 1)

                def values(t, h, p):
                    pe.wait_ge(sig(ph, "lo_pool"), t * HEADS + h + 1)
                    pe.wait_ge(sig(ph, "lo_dve"), t * HEADS + h + 1)
                    g, s = h // HPG, h % HP
                    if h % HPG == 0 and g > 0:
                        pe.wait_ge(sig(ph, "o_read"), t * GROUPS + g)
                    if h == 0:
                        pe.wait_ge(sig(ph, "v_parts"), t + 1)
                    hi = prob_hi(s)
                    for qb in range(BLK):
                        o0 = ((h % HPG) * BLK + qb) * VC
                        dst = ps[:, OB, o0:o0 + VC]
                        c = slice(qb * P, qb * P + P)
                        for kb in range(BLK):
                            v = v_parts[p][:, kb, h]
                            pe.matmul(dst, hi[:, kb, c], v, start=(kb == 0), stop=False)
                            last = pe.matmul(dst, prob_lo[:, s, kb, c], v, start=False, stop=(kb == BLK - 1))
                    last.then_inc(sig(ph, "pv"), 1)

                def head_v(t, p):
                    pe.wait_ge(sig(ph, "x_hi"), t + 1)
                    for b in range(BLK):
                        last = pe.matmul(rows4(MISC)[:, b], xnT[:, b * P:b * P + P], w_v[:], start=True,
                                         stop=True)
                    last.then_inc(sig(ph, "v"), 1)

                def head_qk(t, p, i):
                    if i == 0:
                        pe.wait_ge(sig(ph, "x_lo"), t + 1)
                    three(wide(MISC), w_qk[:, i, 0], w_qk[:, i, 1], xnT_hl[p][:, 0], xnT_hl[p][:, 1])\
                        .then_inc(sig(ph, "qk"), 1)

                def bank_read(name, count):
                    pe.wait_ge(sig(ph, name), count)

                def attended(t):
                    pe.wait_ge(sig(ph, "o_all"), t + 1)
                    for b in range(BLK):
                        last = pe.transpose(rows4(MISC)[:, b], o_all[:, b], ident[:])
                    last.then_inc(sig(ph, "oT"), 1)

                def project(t):
                    pe.wait_ge(sig(ph, "oT_sb"), t + 1)
                    for b in range(BLK):
                        last = pe.matmul(rows4(MISC)[:, b], oT[:, b * P:b * P + P], w_o[:], start=True,
                                         stop=True)
                    last.then_inc(sig(ph, "y"), 1)

                def shifted(t, g, p):
                    pe.wait_ge(sig(ph, "shift"), t * GROUPS + g + 1)
                    queries(t, g, p, "qsh")

                def small_work(t, p, h, more, before):
                    n, q, g4 = t + 1, 1 - p, t * GROUPS
                    if h == 0:
                        bank_read("qsh_sb", g4 + 1)
                        keys(t, 2, p)
                    if h == 1:
                        bank_read("k_pad", g4 + 3)
                        queries(t, 2, p, "qs")
                    if h == 2 and before is not None:
                        project(before)
                    if h == 3:
                        bank_read("qs_sb", g4 + 3)
                        shifted(t, 1, p)
                    if h == 4:
                        if more:
                            bank_read("x_hi", n + 1)
                        else:
                            bank_read("qsh_sb", g4 + 2)
                        keys(t, 3, p)
                    if h == 5:
                        bank_read("k_pad", g4 + 4)
                        queries(t, 3, p, "qs")
                    if h == 6 and more:
                        bank_read("qk_read", n * 4 + 1)
                        head_qk(n, q, 1)
                    if h == 7:
                        if more:
                            bank_read("qk_read", n * 4 + 3)
                        else:
                            bank_read("qs_sb", g4 + 4)
                        shifted(t, 2, p)
                    if h == 9 and more:
                        bank_read("v_part", n * 2 + 1)
                        keys(n, 0, q)
                    if h == 10 and more:
                        bank_read("k_pad", n * GROUPS + 1)
                        queries(n, 0, q, "qs")
                    if h == 11:
                        if more:
                            bank_read("qs_sb", n * GROUPS + 1)
                        else:
                            bank_read("qsh_sb", g4 + 3)
                        shifted(t, 3, p)
                    if h == 12 and more:
                        bank_read("qsh_sb", g4 + 4)
                        keys(n, 1, q)
                    if h == 13 and more:
                        bank_read("k_pad", n * GROUPS + 2)
                        queries(n, 1, q, "qs")
                    if h == 15 and more:
                        bank_read("qs_sb", n * GROUPS + 2)
                        shifted(n, 0, q)

                def late_work(t, p, h, more, before):
                    n, q, g4 = t + 1, 1 - p, t * GROUPS
                    if h == 1 and before is not None:
                        bank_read("qs_sb", g4 + 3)
                        attended(before)
                    if h == 3 and more:
                        bank_read("qsh_sb", g4 + 2)
                        transpose_in(ph, n, MISC)
                    if h == 5 and more:
                        bank_read("qs_sb", g4 + 4)
                        head_qk(n, q, 0)
                    if h == 6 and more:
                        bank_read("qk_read", n * 4 + 2)
                        head_qk(n, q, 2)
                    if h == 7 and more:
                        bank_read("qsh_sb", g4 + 3)
                        head_qk(n, q, 3)
                    if h == 8 and more:
                        bank_read("qk_read", n * 4 + 4)
                        head_v(n, q)

                def step(t, p, h, more, before=None):
                    first = h == 0 and before is None
                    ahead = h + AHEAD
                    scores = ahead < HEADS or more
                    t1, g, j = t + ahead // HEADS, ahead % HEADS // HPG, ahead % HPG
                    pass2(t, h, 0, first)
                    small_work(t, p, h, more, before)
                    if scores:
                        pass1(t1, g, j, (2,))
                    pass2(t, h, 1, first)
                    if scores:
                        pass1(t1, g, j, (3,))
                    if h > 0:
                        values(t, h - 1, p)
                    elif before is not None:
                        values(before, HEADS - 1, 1 - p)
                    pass1_ahead(t, h + 1, more)
                    late_work(t, p, h, more, before)

                def pass1_ahead(t, h, more):
                    ahead = h + AHEAD
                    if ahead < HEADS or more:
                        pass1(t + ahead // HEADS, ahead % HEADS // HPG, ahead % HPG, (0, 1))

                def head(t, p):
                    pe.wait_ge(sig(ph, "weights"), 1)
                    transpose_in(ph, t, MISC)
                    head_v(t, p)
                    bank_read("v_part", 2 * t + 1)
                    head_qk(t, p, 0)
                    for i in range(1, 4):
                        bank_read("qk_read", t * 4 + i)
                        head_qk(t, p, i)
                    bank_read("qk_read", t * 4 + 4)
                    for g in range(2):
                        if g == 1:
                            bank_read("qs_sb", t * GROUPS + 1)
                        keys(t, g, p)
                        bank_read("k_pad", t * GROUPS + g + 1)
                        queries(t, g, p, "qs")
                    bank_read("qs_sb", t * GROUPS + 2)
                    for h in range(AHEAD):
                        if h == HPG:
                            shifted(t, 0, p)
                        pass1(t, h // HPG, h % HPG)
                    pe.wait_ge(sig(ph, "qsh_sb"), t * GROUPS + 1)
                    pass1_ahead(t, 0, True)
                    for h in range(EARLY):
                        step(t, p, h, True)

                def body(t, p, more):
                    for h in range(EARLY, HEADS):
                        step(t, p, h, more)
                    if more:
                        for h in range(EARLY):
                            step(t + 1, 1 - p, h, two_more(t), before=t)
                    else:
                        values(t, HEADS - 1, p)
                        attended(t)
                        project(t)
                over_tiles(pe, ph, head, body)

            pe.wait_ge(consts, 16 * 16)
            pe.wait_ge(setup, 3)
            ffn0(0)
            barrier(pe, 1)
            attention0()
            barrier(pe, 2)
            ffn0(2)
            barrier(pe, 3)
            ffn1(3)
            barrier(pe, 4)
            attention1()
            barrier(pe, 5)
            ffn1(5)
            barrier(pe, 6)


def kernel(**inputs):
    import concourse.bacc as _bacc
    from concourse.bass_utils import run_bass_kernel_spmd as _run

    def a(name):
        return np.asarray(inputs[name])

    qkv = a("L1_attn_w_qkv").reshape(D, 3, HEADS, HD // 2, 2)
    swapped = qkv[..., ::-1]
    w_qk = np.stack([qkv[:, 1], swapped[:, 1], qkv[:, 0], swapped[:, 0]], axis=1).reshape(D, 4 * P)
    data = {
        "x": a("L0_attn_x"), "gate_w": a("L0_ffn_Wg"), "gate_b": a("L0_ffn_bg"),
        "b1": a("L0_ffn_b1"), "b2": a("L0_ffn_b2").reshape(1, E0 * D),
        "W1": a("L0_ffn_W1").transpose(1, 0, 2).reshape(D, E0 * FF0),
        "W2": a("L0_ffn_W2").reshape(E0, FB0, P, D).transpose(2, 1, 0, 3).reshape(P, FB0 * E0 * D),
        "qkv_wT": a("L0_attn_qkv_w").T, "out_wT": a("L0_attn_out_w").T,
        "out_b0": a("L0_attn_out_b"), "temp": a("L0_attn_temp").reshape(HEADS),
        "selT": a("L1_ffn_expert_sel").T,
        "keys": a("L1_ffn_keys").transpose(1, 0, 2).reshape(D, E1 * FF1),
        "values": a("L1_ffn_values").reshape(FB1, P, D).transpose(1, 0, 2).reshape(P, FB1 * D),
        "w_qk": w_qk, "w_v": qkv[:, 2].reshape(D, P), "w_o": a("L1_attn_w_proj"),
        "out_b1": a("L1_attn_b_proj"),
    }
    data.update({f"c_{k}": v for k, v in token_constants().items()})
    nc = _bacc.Bacc("TRN2", target_bir_lowering=False, num_devices=1)
    arrays, d = {}, {}
    for name, v in data.items():
        v = np.ascontiguousarray(v)
        arrays[f"in_{name}"] = v
        d[name] = nc.dram_tensor(f"in_{name}", v.shape, mybir.dt.from_np(v.dtype), kind="ExternalInput").ap()
    out = nc.dram_tensor("out_0", (BATCH, SEQ, D), F32, kind="ExternalOutput").ap()
    const = {k[2:]: v for k, v in d.items() if k.startswith("c_")}
    weights = dict(
        gate_w=d["gate_w"], gate_b=d["gate_b"], b1=d["b1"], b2=d["b2"], router1=d["selT"],
        qkv_w=d["qkv_wT"], out_w=d["out_wT"], out_b0=d["out_b0"], temp=d["temp"],
        w_v=d["w_v"], w_o=d["w_o"], out_b1=d["out_b1"],
        staged=[
            (const["sel_expert"], E0 * P),
            (d["W1"], E0 * FF0),
            (d["W2"], FB0 * E0 * D),
            (const["sel_gate"], FB1 * P),
            (d["keys"], E1 * FF1),
            (d["values"], FB1 * D),
        ],
        staged_late=[(const["stack"], GROUPS * 4 * P), (d["w_qk"], 4 * P)],
    )
    macaron(nc, d["x"], weights, const, out)
    r = _run(nc, [arrays], core_ids=[0])
    return r.results[0]["out_0"]
```

```python
from contextlib import ExitStack

import numpy as np

import concourse.bass as bass
from concourse import mybir

ALU = mybir.AluOpType
ACT = mybir.ActivationFunctionType
AXX = mybir.AxisListType.X
F32 = mybir.dt.float32
F32R = mybir.dt.float32r
BF16 = mybir.dt.bfloat16
FP16 = mybir.dt.float16

P = 128
D = 128
BATCH, SEQ = 16, 512
BLK = SEQ // P
TILES = BATCH
PAIRS = TILES // 2
HEADS, HD = 16, 8
E0, FF0 = 4, 512
FB0 = FF0 // P
E1, FF1 = 32, 64
FB1 = E1 * FF1 // P
PER1 = P // FF1
TOP1 = 4
LEAD = 4
RING1 = 8
BIG = 3.0e38
LN_EPS = 1e-5
GROUPS, HPG = 4, 4
VC = 3 * HD + 1
SCALE = HD ** -0.5
POOL_FB = (2, 5, 8, 11, 14)
POOL_KB = 2
AHEAD = 5
EARLY = 3
FIRST = (0, 0, TILES, 0, 0, TILES)
KIND = (0, 1, 0, 3, 4, 3)
HP = 2


def token_constants():
    c = {}
    c["ident"] = np.eye(P, dtype=np.float32)
    s = np.zeros((P, E0, P), np.float32)
    for e in range(E0):
        s[e, e, :] = 1
    c["sel_expert"] = s.reshape(P, -1)
    s = np.zeros((P, FB1, P), np.float32)
    for part in range(3):
        for e in range(E1):
            s[part * E1 + e, e // PER1, (e % PER1) * FF1:(e % PER1 + 1) * FF1] = 1
    c["sel_gate"] = s.reshape(P, -1)
    small = np.zeros((P, 64), np.float32)
    small[0:4, 0] = small[4:8, 1] = small[8:12, 2] = 1
    small[0, 3] = small[1, 4] = small[2, 5] = 1
    small[:, 6:10] = [4, 3, 2, 1]
    for j in range(HPG):
        small[32 * j + 3 * HD, 10] = 1
    for ch in range(P):
        small[ch, 16 + ch // HD] = 1
    small[0:3, 11] = 1
    c["small"] = small
    s = np.zeros((P, P), np.float32)
    for ch in range(P):
        s[ch // HD, ch] = 1
    c["head_rows"] = s
    s = np.zeros((P, GROUPS, 4, P), np.float32)
    for g in range(GROUPS):
        for j in range(HPG):
            for d in range(HD):
                ch, r = (HPG * g + j) * HD + d, 32 * j + d
                s[ch, g, 0, r] = s[ch, g, 0, r + HD] = 1
                s[ch, g, 1, r + 2 * HD] = 1
                s[ch, g, 2, r] = s[ch, g, 2, r + 2 * HD] = 1
                s[ch, g, 3, r + HD] = 1
    c["stack"] = s.reshape(P, -1)
    theta = (np.float32(1.0) / np.float32(10000.0) ** (np.arange(0, HD, 2, dtype=np.float32) / np.float32(HD))
             * np.float32(3.0)).astype(np.float32)
    ang = (np.arange(SEQ, dtype=np.float32)[:, None] * theta[None, :]).astype(np.float32)
    cos, sin = np.cos(ang.astype(np.float64)), np.sin(ang.astype(np.float64))
    col = np.arange(SEQ)
    pos = BLK * (col % P) + col // P
    ch = np.arange(P) % HD
    sign = np.where(ch % 2 == 0, -1.0, 1.0)[:, None]
    c["cos"] = np.ascontiguousarray(cos[pos][:, ch // 2].T.astype(np.float32))
    c["sin"] = np.ascontiguousarray((sin[pos][:, ch // 2].T * sign).astype(np.float32))
    return c


def macaron(nc, x_in, w, const, out):
    whole = ExitStack()
    with whole:
        def sem(name):
            return whole.enter_context(nc.semaphore(name))

        def persistent(name, shape, dt=F32):
            return whole.enter_context(nc.sbuf_tensor(name, shape, dt))

        ps = whole.enter_context(nc.psum_tensor("ps", [P, 8, 512], F32))

        x = persistent("x", [P, TILES * BLK, D])
        ident = persistent("ident", [P, P])
        ident_b = persistent("ident_b", [P, P], BF16)
        small = persistent("small", [P, 64])
        neg_half = persistent("neg_half", [P, BLK])
        keys_hl = persistent("keys_hl", [P, 2, E1 * FF1], F32R)
        vals_hl = persistent("vals_hl", [P, 2, FB1, D], F32R)
        sel_gate = persistent("sel_gate", [P, FB1, P], BF16)
        router1 = persistent("router1", [P, E1])
        xn = persistent("xn", [P, BLK, D])
        xnT = persistent("xnT", [P, SEQ])
        xnT_hl = [persistent(f"xnT_hl{b}", [P, 2, SEQ], F32R) for b in range(2)]
        stats = persistent("stats", [P, BLK, 6])
        meanvar = persistent("meanvar", [P, BLK, 2])
        var_eps = persistent("var_eps", [P, BLK])
        rstd = persistent("rstd", [P, BLK])

        early = ExitStack()

        def early_sb(name, shape, dt=F32):
            return early.enter_context(nc.sbuf_tensor(name, shape, dt))

        stage = [early_sb(f"stage{b}", [P, 2048]) for b in range(2)]
        w1_hl = early_sb("w1_hl", [P, 2, E0, FF0], F32R)
        w2_hl = early_sb("w2_hl", [P, 2, FB0, E0 * D], F32R)
        sel_expert = early_sb("sel_expert", [P, E0, P], BF16)
        gate_w = early_sb("gate_w", [P, E0])
        gate_b = early_sb("gate_b", [P, E0])
        bias_m = early_sb("bias_m", [P, 2, 512], BF16)
        ones3 = early_sb("ones3", [P, P], BF16)
        logit = early_sb("logit", [P, BLK, E0])
        best = early_sb("best", [P, BLK])
        equal = early_sb("equal", [P, BLK, E0])
        first = early_sb("first", [P, BLK])
        onehot = early_sb("onehot", [P, BLK, 3 * E0], BF16)
        half_hot = [early_sb(f"half_hot{b}", [P, BLK, E0]) for b in range(2)]
        onehotT = [early_sb(f"onehotT{b}", [P, SEQ], BF16) for b in range(2)]
        qkv_f = early_sb("qkv_f", [P, 2, P])
        qkvT_hl = early_sb("qkvT_hl", [P, 2, P], F32R)
        out_b0 = early_sb("out_b0", [P, D])
        temp_b = early_sb("temp_b", [P, HEADS])
        temp_ind = early_sb("temp_ind", [P, HEADS])
        head_rows = early_sb("head_rows", [P, P])

        with ExitStack() as once_own:
            bias_f = once_own.enter_context(nc.sbuf_tensor("bias_f", [P, 2, 512], F32))
            bias_p = once_own.enter_context(nc.sbuf_tensor("bias_p", [P, 3, 2, 512], BF16))
            bias_r = once_own.enter_context(nc.sbuf_tensor("bias_r", [P, 2, 2, 512], F32))

        ffn0_own = ExitStack()

        def ffn0_sb(name, shape, dt=F32):
            return ffn0_own.enter_context(nc.sbuf_tensor(name, shape, dt))

        x_masked = [ffn0_sb(f"x_masked{b}", [P, E0, 2, SEQ], F32R) for b in range(2)]
        g32 = ffn0_sb("g32", [P, FB0, SEQ])
        g_hi = ffn0_sb("g_hi", [P, FB0, SEQ], F32R)
        g_lo = ffn0_sb("g_lo", [P, FB0, SEQ], F32R)
        ffn0_own.close()
        att0_own = ExitStack()

        def att0_sb(name, shape, dt=F32):
            return att0_own.enter_context(nc.sbuf_tensor(name, shape, dt))

        w32 = [att0_sb(f"w32_{b}", [P, SEQ]) for b in range(4)]
        wsq = [att0_sb(f"wsq{b}", [P, SEQ]) for b in range(4)]
        norm2 = att0_sb("norm2", [P, 1])
        inv2 = att0_sb("inv2", [P, 1])
        norm_ind = att0_sb("norm_ind", [P, HEADS])
        smax = att0_sb("smax", [P, BLK])
        sexp = att0_sb("sexp", [P, BLK, HEADS])
        ssum = att0_sb("ssum", [P, BLK])
        pi = [att0_sb(f"pi{b}", [P, BLK, P]) for b in range(2)]
        piT = att0_sb("piT", [P, SEQ])
        pi_rows = att0_sb("pi_rows", [P, SEQ])
        pi_sum = att0_sb("pi_sum", [P, 1])
        prod = att0_sb("prod", [P, SEQ])
        dots = att0_sb("dots", [P, 4])
        outT = att0_sb("outT", [P, SEQ])
        att0_own.close()
        early.close()

        def ffn1_memory():
            with ExitStack() as own:
                def sb(name, shape, dt=F32):
                    return own.enter_context(nc.sbuf_tensor(name, shape, dt))
                m = dict(
                    logit=sb("logit1", [P, BLK, E1]), top8=sb("top8", [P, BLK, 8]),
                    taken=sb("taken", [P, BLK, E1]), sig=sb("sig", [P, BLK, E1]),
                    gate=sb("gate", [P, BLK, E1]), rest=sb("rest", [P, 2, BLK, E1]),
                    parts=sb("parts", [P, BLK, 3 * E1], BF16),
                    gateT=[sb(f"gateT{b}", [P, SEQ], BF16) for b in range(2)],
                    relu=sb("relu", [P, 4, SEQ]), m32=sb("m32", [P, RING1, SEQ]),
                    hi=sb("hi", [P, RING1, SEQ], F32R), lo=sb("lo", [P, RING1, SEQ], F32R),
                    yT=sb("yT", [P, SEQ]))
            return m

        ffn1_mem = ffn1_memory()

        late = ExitStack()

        def late_sb(name, shape, dt=F32):
            return late.enter_context(nc.sbuf_tensor(name, shape, dt))

        w_qk = late_sb("w_qk", [P, 4, 2, P], F32R)
        w_v = late_sb("w_v", [P, P])
        w_o = late_sb("w_o", [P, P])
        out_b1 = late_sb("out_b1", [P, D])
        stack_sel = late_sb("stack_sel", [P, GROUPS, 4, P], F32R)
        cos_t = late_sb("cos_t", [P, SEQ])
        sin_t = late_sb("sin_t", [P, SEQ])
        rope = late_sb("rope", [P, 3, SEQ])
        qk_hl = [late_sb(f"qk_hl{b}", [P, 2, 2, SEQ], F32R) for b in range(2)]
        ident_r = late_sb("ident_r", [P, P], F32R)
        k_pad = late_sb("k_pad", [P, HEADS, SEQ], F32R)
        q_st = late_sb("q_st", [P, 2, SEQ], F32R)
        q_sh = late_sb("q_sh", [P, 2, SEQ], F32R)
        qmax = late_sb("qmax", [P, 2, HPG, BLK])
        shift = late_sb("shift", [P, 2, BLK, P], F32R)
        with ExitStack() as once_own:
            stage_l = [once_own.enter_context(nc.sbuf_tensor(f"stage_l{b}", [P, 2048], F32)) for b in range(2)]
        prob = late_sb("prob", [P, HP, BLK, SEQ])
        prob_lo = late_sb("prob_lo", [P, HP, BLK, SEQ], FP16)
        v32 = late_sb("v32", [P, BLK, D])
        vrest = late_sb("vrest", [P, 2, BLK, D])
        v_parts = [late_sb(f"v_parts{b}", [P, BLK, HEADS, VC], BF16) for b in range(2)]
        o_sum = late_sb("o_sum", [P, HPG * BLK, HD])
        o_rcp = late_sb("o_rcp", [P, HPG * BLK])
        o_all = late_sb("o_all", [P, BLK, D])
        oT = late_sb("oT", [P, SEQ])
        late.close()

        x_first, x_rest, w_in, stage_free = sem("x_first"), sem("x_rest"), sem("w_in"), sem("stage_free")
        consts, setup = sem("consts"), sem("setup")
        early_in, bias_in = sem("early_in"), sem("bias_in")
        phase_end = sem("phase_end")
        stored = sem("stored")
        signals = {}

        def sig(ph, name):
            ph = KIND[ph]
            if (ph, name) not in signals:
                signals[ph, name] = sem(f"{name}_{ph}")
            return signals[ph, name]

        class Chain:

            def __init__(self, eng, s, per_tile):
                self.eng, self.s, self.per, self.n, self.t = eng, s, per_tile, 0, 0

            def tile(self, t):
                assert self.n in (0, self.per), (self.n, self.per, self.s)
                self.t, self.n = t, 0

            def step(self, ins):
                self.n += 1
                return ins.then_inc(self.s, 1)

            def settle(self):
                self.eng.wait_ge(self.s, self.t * self.per + self.n)

            def settle_alone(self):
                pass_wait(self.eng, self.s, self.t * self.per + self.n)

        passed = {}

        def pass_wait(eng, s, value):
            if eng not in passed:
                passed[eng] = sem(f"passed{len(passed)}")
            eng.wait_ge(s, value)
            eng.sem_inc(passed[eng], 1)

        def over_tiles(eng, ph, head, body):
            t0 = FIRST[ph]
            head(t0, 0)
            with eng.Fori(t0 // 2, t0 // 2 + PAIRS - 1) as pair:
                body(pair * 2, 0, True)
                body(pair * 2 + 1, 1, True)
            body(t0 + TILES - 2, 0, True)
            body(t0 + TILES - 1, 1, False)

        def three_deep(eng, step):
            def run(t, k):
                step(t, k, lambda n: not isinstance(t, int) or 0 <= t + n < TILES)
            for t in range(-2, 2):
                run(t, t % 4)
            with eng.Fori(1, TILES // 4 - 1) as g:
                for j in range(4):
                    run(g * 4 + (j - 2), (j - 2) % 4)
            for t in range(TILES - 6, TILES + 1):
                run(t, t % 4)

        def two_more(t):
            return not isinstance(t, int)

        def barrier(eng, n):
            eng.drain().then_inc(phase_end, 1)
            eng.wait_ge(phase_end, 4 * n)

        FFN1_PH = (3, 5)
        TR, SM = 0, 1
        MASK, H0, Y0 = 2, 4, 6
        G1, H1, Y1 = 2, 4, 7
        h1_bank = [4, 5, 6] * 5 + [5]
        h1_since = [4, 2, 4] + [3] * 12 + [2]
        WT, SC, PT, PR, YA = 1, 2, 3, 4, 5
        PASS1, PASS2, OB, MISC = 0, 2, 6, 7

        def prob_hi(s):
            return prob[:, s].bitcast(BF16).rearrange("p b (n two) -> p b n two", two=2)[:, :, :, 1]

        def wide(bank, rows=P, dt=F32):
            v = ps[0:rows, bank, :]
            return v if dt == F32 else v.bitcast(dt)

        def rows4(bank):
            return ps[:, bank, :].rearrange("p (b n) -> p b n", b=BLK)

        block = whole.enter_context(nc.Block())
        views = w

        staged = [(v, n) for v, n in views["staged"]]

        @block.sync
        def _(sp):
            xv = x_in.rearrange("t (p b) d -> p t b d", p=P)
            xs = x[:, :, :].rearrange("p (t b) d -> p t b d", b=BLK)
            sp.dma_start(xs[:, 0:2], xv[:, 0:2]).then_inc(x_first, 16)
            sp.dma_start(ident[:], const["ident"]).then_inc(early_in, 16)
            sp.dma_start(small[:], const["small"]).then_inc(early_in, 16)
            sp.dma_start(gate_w[:], views["gate_w"]).then_inc(early_in, 16)
            sp.dma_start(gate_b[:], views["gate_b"].partition_broadcast(P)).then_inc(early_in, 16)
            for n in range(2):
                sp.dma_start(stage[n][:, 0:staged[n][1]], staged[n][0]).then_inc(w_in, 16)
            sp.wait_ge(setup, 1)
            for part in range(3):
                sp.dma_start(bias_f[E0 * part:E0 * part + E0, 0, :], views["b1"]).then_inc(bias_in, 16)
                sp.dma_start(bias_f[part:part + 1, 1, :], views["b2"]).then_inc(bias_in, 16)
            sp.wait_ge(w_in, 16 * 2)
            for n, (v, cols) in enumerate(staged):
                if n >= 2:
                    sp.wait_ge(stage_free, n - 1)
                    sp.dma_start(stage[n % 2][:, 0:cols], v).then_inc(w_in, 16)
                    if n == 2:
                        sp.dma_start(xs[:, 2:TILES], xv[:, 2:TILES]).then_inc(x_rest, 16)
                        sp.dma_start(router1[:], views["router1"]).then_inc(consts, 16)
                        sp.dma_start(qkv_f[:, 0, :], views["qkv_w"]).then_inc(consts, 16)
                        sp.dma_start(qkv_f[:, 1, :], views["out_w"]).then_inc(consts, 16)
                        sp.dma_start(out_b0[:], views["out_b0"].partition_broadcast(P)).then_inc(consts, 16)
                        sp.dma_start(temp_b[:], views["temp"].partition_broadcast(P)).then_inc(consts, 16)
                        sp.dma_start(head_rows[:], const["head_rows"]).then_inc(consts, 16)
                    sp.wait_ge(w_in, 16 * (n + 1))
            sp.wait_ge(phase_end, 4 * 4)
            for n, (dst, src) in enumerate([
                    (w_v[:], views["w_v"]), (w_o[:], views["w_o"]),
                    (out_b1[:], views["out_b1"].partition_broadcast(P)),
                    (cos_t[:], const["cos"]), (sin_t[:], const["sin"])]):
                sp.dma_start(dst, src).then_inc(sig(4, "tables"), 16)
            for n, (v, cols) in enumerate(views["staged_late"]):
                m = n + len(staged)
                sp.dma_start(stage_l[n][:, 0:cols], v).then_inc(w_in, 16)
                sp.wait_ge(w_in, 16 * (m + 1))
            ov = out.rearrange("t (p b) d -> p t b d", p=P)
            with sp.Fori(0, TILES) as t:
                sp.wait_ge(sig(5, "x_done"), (t + TILES) * 4 + 4)
                sp.dma_start(ov[:, bass.ds(t, 1)], xs[:, bass.ds(t, 1)]).then_inc(stored, 16)
            sp.wait_ge(stored, 16 * TILES)

        @block.gpsimd
        def _(pool):
            pool.memset(neg_half[:], -0.5)
            pool.memset(ones3[:], 0.0)
            pool.memset(bias_f[:], 0.0).then_inc(setup, 1)
            for b in range(2):
                last = pool.memset(onehotT[b][:], 0.0)
            last.then_inc(setup, 1)

            def rstd_of(ph):
                def head(t, p):
                    ve = sig(ph, "var_eps")
                    pass_wait(pool, sig(ph, "meanvar"), t + 1)
                    pool.tensor_scalar(var_eps[:], meanvar[:, :, 1], LN_EPS, None, ALU.add).then_inc(ve, 1)
                    pool.wait_ge(ve, t + 1)
                    pool.tensor_tensor(rstd[:], var_eps[:], neg_half[:], ALU.pow).then_inc(sig(ph, "rstd"), 1)
                return head

            def low_parts(ph, m):
                def step(t, fb, more):
                    if fb == LEAD and more:
                        rstd_of(ph)(t + 1, 0)
                    if fb in POOL_FB:
                        pool.wait_ge(sig(ph, "hi"), t * FB1 + fb + 1)
                        s = fb % RING1
                        pool.tensor_tensor(m["lo"][:, s], m["m32"][:, s], m["hi"][:, s].bitcast(F32),
                                           ALU.subtract).then_inc(sig(ph, "lo_pool"), 1)

                def head(t, p):
                    rstd_of(ph)(t, p)
                    for fb in range(LEAD):
                        step(t, fb, True)

                def body(t, p, more):
                    for fb in range(LEAD, FB1):
                        step(t, fb, more)
                    for fb in range(LEAD if more else 0):
                        step(t + 1, fb, True)
                return head, body

            for ph in range(3):
                if ph == 1:
                    for b in range(2):
                        last = pool.memset(pi[b][:], 0.0)
                    last.then_inc(sig(1, "zeroed"), 1)
                with pool.Fori(FIRST[ph], FIRST[ph] + TILES) as t:
                    rstd_of(ph)(t, 0)
                    if ph == 1:
                        pool.wait_ge(sig(1, "xn"), t + 1)
                        xt = x[:, bass.ds(t * BLK, BLK), :]
                        pool.tensor_tensor(xt, xt, out_b0[:].unsqueeze(1).broadcast_to([P, BLK, D]),
                                           ALU.add).then_inc(sig(1, "biased"), 1)
                barrier(pool, ph + 1)
            for ph in (3, 4, 5):
                if ph in FFN1_PH:
                    m = ffn1_mem
                    for b in range(2):
                        last = pool.memset(m["gateT"][b][:], 0.0)
                    last.then_inc(sig(ph, "zeroed"), 1)
                    over_tiles(pool, ph, *low_parts(ph, m))
                else:
                    def bias(t):
                        pool.wait_ge(sig(4, "xn"), t + 1)
                        xt = x[:, bass.ds(t * BLK, BLK), :]
                        pool.tensor_tensor(xt, xt, out_b1[:].unsqueeze(1).broadcast_to([P, BLK, D]),
                                           ALU.add).then_inc(sig(4, "biased"), 1)

                    def x_low(t, p):
                        pool.wait_ge(sig(4, "x_hi"), t + 1)
                        pool.tensor_tensor(xnT_hl[p][:, 1, :], xnT[:], xnT_hl[p][:, 0, :].bitcast(F32),
                                           ALU.subtract).then_inc(sig(4, "x_lo"), 1)

                    def rope_sum(t, a):
                        if a == 1:
                            pool.wait_ge(sig(4, "qk_hl"), t * 2 + 1)
                        pool.wait_ge(sig(4, "qk_read"), t * 4 + 2 * a + 2)
                        pool.tensor_tensor(rope[:, 2], rope[:, 0], rope[:, 1],
                                           ALU.add).then_inc(sig(4, "rope_sum"), 1)

                    def rope_low(t, p, a):
                        pool.wait_ge(sig(4, "qk_hi"), t * 2 + a + 1)
                        pool.tensor_tensor(qk_hl[p][:, a, 1], rope[:, 2], qk_hl[p][:, a, 0].bitcast(F32),
                                           ALU.subtract).then_inc(sig(4, "qk_hl"), 1)

                    def value_rest(t, p, i):
                        pool.wait_ge(sig(4, "v_part"), t * 2 + i + 1)
                        parts = v_parts[p][:, :, :, HD * i:HD * i + HD]
                        cur = v32 if i == 0 else vrest[:, 0]
                        pool.tensor_tensor(vrest[:, i].rearrange("p b (h d) -> p b h d", d=HD),
                                           cur[:].rearrange("p b (h d) -> p b h d", d=HD), parts,
                                           ALU.subtract).then_inc(sig(4, "v_rest"), 1)

                    def step4(t, p, h, more):
                        n, q = t + 1, 1 - p
                        if h == 1 and more:
                            rstd_of(4)(n, q)
                        if h == 3 and more:
                            bias(n)
                        if h in (6, 8) and more:
                            rope_sum(n, h // 8)
                        pool.wait_ge(sig(4, "prob"), t * 2 * HEADS + 2 * h + 2)
                        s, kb = h % HP, slice(BLK - POOL_KB, BLK)
                        pool.tensor_tensor(prob_lo[:, s, kb], prob[:, s, kb], prob_hi(s)[:, kb],
                                           ALU.subtract).then_inc(sig(4, "lo_pool"), 1)
                        if h == 4 and more:
                            x_low(n, q)
                        if h in (7, 8) and more:
                            rope_low(n, q, h - 7)
                        if h in (9, 12) and more:
                            value_rest(n, q, (h - 9) // 3)

                    def head4(t, p):
                        rstd_of(4)(t, p)
                        pool.memset(shift[:].bitcast(F32), 0.0)
                        for b in range(2):
                            pool.memset(v_parts[b][:, :, :, VC - 1:VC], 1.0)
                        pool.wait_ge(sig(4, "tables"), 16 * 5)
                        bias(t)
                        x_low(t, p)
                        for a in range(2):
                            rope_sum(t, a)
                            rope_low(t, p, a)
                        pool.memset(k_pad[:].bitcast(F32), 0.0).then_inc(sig(4, "zeroed"), 1)
                        for i in range(2):
                            value_rest(t, p, i)
                        for h in range(EARLY):
                            step4(t, p, h, True)

                    def body4(t, p, more):
                        for h in range(EARLY, HEADS):
                            step4(t, p, h, more)
                        if more:
                            for h in range(EARLY):
                                step4(t + 1, 1 - p, h, two_more(t))

                    over_tiles(pool, 4, head4, body4)
                barrier(pool, ph + 1)

        @block.scalar
        def _(act):
            def copy(o, i):
                return act.activation(o, i, ACT.Copy)

            def transposed(ph, t, p):
                act.wait_ge(sig(ph, "tr"), t + 1)
                copy(xnT[:], wide(TR)).then_inc(sig(ph, "xnT"), 1)
                copy(xnT_hl[p][:, 0, :], wide(TR)).then_inc(sig(ph, "x_hi"), 1)

            def ffn0(ph):
                def hot(t, p):
                    act.wait_ge(sig(ph, "hotT"), t + 1)
                    src = wide(SM, dt=BF16)[0:3 * E0, 512:1024]
                    copy(onehotT[p][0:3 * E0, :], src).then_inc(sig(ph, "onehotT"), 1)

                def head(t, p):
                    transposed(ph, t, p)
                    if ph == 0:
                        act.wait_ge(setup, 2)
                    hot(t, p)

                def body(t, p, more):
                    for fb in range(FB0):
                        act.wait_ge(sig(ph, "h"), t * FB0 + fb + 1)
                        act.activation(g32[:, fb, :], wide(H0 + fb % 2), ACT.Gelu).then_inc(sig(ph, "gelu"), 1)
                        act.wait_ge(sig(ph, "gelu"), t * FB0 + fb + 1)
                        copy(g_hi[:, fb, :], g32[:, fb, :]).then_inc(sig(ph, "g_hi"), 1)
                        if fb == 2 and more:
                            transposed(ph, t + 1, 1 - p)
                    if more:
                        hot(t + 1, 1 - p)
                over_tiles(act, ph, head, body)

            def ffn1(ph):
                m = ffn1_mem

                def sigmoid(t, p):
                    act.wait_ge(sig(ph, "logit"), t + 1)
                    act.activation(m["sig"][:], m["logit"][:], ACT.Sigmoid).then_inc(sig(ph, "sigm"), 1)

                def gateT(t, p):
                    act.wait_ge(sig(ph, "gT"), t + 1)
                    copy(m["gateT"][p][0:3 * E1, :], wide(TR, dt=BF16)[0:3 * E1, 0:512])\
                        .then_inc(sig(ph, "gateT"), 1)

                def high(t, fb):
                    act.wait_ge(sig(ph, "m"), t * FB1 + fb + 1)
                    copy(m["hi"][:, fb % RING1], m["m32"][:, fb % RING1]).then_inc(sig(ph, "hi"), 1)

                def y_out(t):
                    act.wait_ge(sig(ph, "y"), t + 1)
                    copy(m["yT"][:], wide(Y1)).then_inc(sig(ph, "yT"), 1)

                def step(t, p, fb, more, before=None):
                    act.wait_ge(sig(ph, "h"), t * FB1 + fb + 1)
                    act.activation(m["relu"][:, fb % 4, :], wide(h1_bank[fb]), ACT.Relu)\
                       .then_inc(sig(ph, "relu"), 1)
                    if fb > 0:
                        high(t, fb - 1)
                    elif before is not None:
                        high(before, FB1 - 1)
                    if more and fb == 8:
                        transposed(ph, t + 1, 1 - p)
                    if more and fb == 9:
                        sigmoid(t + 1, 1 - p)
                    if more and fb == 15:
                        gateT(t + 1, 1 - p)

                def head(t, p):
                    transposed(ph, t, p)
                    sigmoid(t, p)
                    act.wait_ge(sig(ph, "zeroed"), 1 + FIRST[ph] // TILES)
                    gateT(t, p)
                    for fb in range(LEAD):
                        step(t, p, fb, True)

                def body(t, p, more):
                    for fb in range(LEAD, FB1):
                        step(t, p, fb, more)
                    if more:
                        for fb in range(LEAD):
                            if fb == LEAD - 1:
                                y_out(t)
                            step(t + 1, 1 - p, fb, True, before=t)
                    else:
                        high(t, FB1 - 1)
                        y_out(t)
                over_tiles(act, ph, head, body)

            def attention0():
                ph = 1

                def step(t, k, here):
                    if here(0):
                        act.wait_ge(sig(ph, "piT"), t + 1)
                        copy(piT[:], wide(PT)).then_inc(sig(ph, "piT_sb"), 1)
                    if here(1):
                        act.wait_ge(sig(ph, "s_shift"), t + 2)
                        act.activation(sexp[:], sexp[:], ACT.Exp).then_inc(sig(ph, "s_exp"), 1)
                    if here(2):
                        transposed(ph, t + 2, k % 2)
                    if here(0):
                        act.wait_ge(sig(ph, "pi_rows"), t + 1)
                        act.activation(pi_rows[:], wide(PR), ACT.Copy, accum_out=pi_sum[:])\
                           .then_inc(sig(ph, "pi_sum"), 1)
                    if here(2):
                        act.wait_ge(sig(ph, "w"), t + 3)
                        a = (k + 2) % 4
                        act.activation(wsq[a][:], wide(WT), ACT.Square, accum_out=norm2[:])\
                           .then_inc(sig(ph, "wsq"), 1)
                        copy(w32[a][:], wide(WT)).then_inc(sig(ph, "w32"), 1)
                three_deep(act, step)

            def attention1():
                ph = 4
                one_row = small[:, 10:11]

                def queries(t, g, dst, name):
                    act.wait_ge(sig(ph, name), t * GROUPS + g + 1)
                    copy(dst, wide(MISC)).then_inc(sig(ph, name + "_sb"), 1)

                def key_pads(t, g):
                    act.wait_ge(sig(ph, "ks"), t * GROUPS + g + 1)
                    for j in range(HPG):
                        r = slice(32 * j, 32 * j + 32)
                        last = act.activation(k_pad[r, HPG * g + j, :], ps[r, MISC, :], ACT.Identity,
                                              bias=one_row[r])
                    last.then_inc(sig(ph, "k_pad"), 1)

                def head_a(t, p):
                    act.wait_ge(sig(ph, "tr"), t + 1)
                    copy(xnT[:], wide(MISC)).then_inc(sig(ph, "xnT"), 1)
                    copy(xnT_hl[p][:, 0, :], wide(MISC)).then_inc(sig(ph, "x_hi"), 1)

                def head_b(t, p):
                    act.wait_ge(sig(ph, "v"), t + 1)
                    copy(v32[:], rows4(MISC)).then_inc(sig(ph, "v32"), 1)
                    part(t, p, 0)

                def part(t, p, i):
                    if i > 0:
                        act.wait_ge(sig(ph, "v_rest"), 2 * t + i)
                    else:
                        act.wait_ge(sig(ph, "v32"), t + 1)
                    src = v32 if i == 0 else vrest[:, i - 1]
                    copy(v_parts[p][:, :, :, HD * i:HD * i + HD], src[:].rearrange("p b (h d) -> p b h d", d=HD))\
                        .then_inc(sig(ph, "v_part" if i < 2 else "v_parts"), 1)

                def rope_high(t, p, a):
                    act.wait_ge(sig(ph, "rope_sum"), t * 2 + a + 1)
                    copy(qk_hl[p][:, a, 0], rope[:, 2]).then_inc(sig(ph, "qk_hi"), 1)

                def exps(t, h):
                    s = h % HP
                    for half in range(2):
                        act.wait_ge(sig(ph, "st"), t * 2 * HEADS + 2 * h + half + 1)
                        b0 = PASS2 + 2 * half
                        act.activation(prob[:, s, 2 * half:2 * half + 2, :], ps[:, b0:b0 + 2, :], ACT.Exp,
                                       scale=SCALE).then_inc(sig(ph, "prob"), 1)

                def project(t):
                    act.wait_ge(sig(ph, "oT"), t + 1)
                    copy(oT[:], wide(MISC)).then_inc(sig(ph, "oT_sb"), 1)

                def step(t, p, h, more, before=None):
                    n, q = t + 1, 1 - p
                    exps(t, h)
                    if h == 0:
                        key_pads(t, 2)
                    if h == 1:
                        queries(t, 2, q_st[:, 0, :], "qs")
                        if before is not None:
                            project(before)
                    if h == 3:
                        queries(t, 1, q_sh[:, 1, :], "qsh")
                    if h == 3 and more:
                        head_a(n, q)
                    if h == 4:
                        key_pads(t, 3)
                    if h == 5:
                        queries(t, 3, q_st[:, 1, :], "qs")
                    if h == 7:
                        queries(t, 2, q_sh[:, 0, :], "qsh")
                    if h in (7, 8) and more:
                        rope_high(n, q, h - 7)
                    if h == 8 and more:
                        head_b(n, q)
                    if h == 9 and more:
                        key_pads(n, 0)
                    if h == 10 and more:
                        queries(n, 0, q_st[:, 0, :], "qs")
                    if h == 11:
                        queries(t, 3, q_sh[:, 1, :], "qsh")
                        if more:
                            part(n, q, 1)
                    if h == 12 and more:
                        key_pads(n, 1)
                    if h == 13 and more:
                        queries(n, 1, q_st[:, 1, :], "qs")
                    if h == 14 and more:
                        part(n, q, 2)
                    if h == 15 and more:
                        queries(n, 0, q_sh[:, 0, :], "qsh")

                def head(t, p):
                    head_a(t, p)
                    head_b(t, p)
                    for a in range(2):
                        rope_high(t, p, a)
                    for i in (1, 2):
                        part(t, p, i)
                    act.wait_ge(sig(ph, "zeroed"), 1)
                    key_pads(t, 0)
                    queries(t, 0, q_st[:, 0, :], "qs")
                    key_pads(t, 1)
                    queries(t, 1, q_st[:, 1, :], "qs")
                    queries(t, 0, q_sh[:, 0, :], "qsh")
                    for h in range(EARLY):
                        step(t, p, h, True)

                def body(t, p, more):
                    for h in range(EARLY, HEADS):
                        step(t, p, h, more)
                    if more:
                        for h in range(EARLY):
                            step(t + 1, 1 - p, h, two_more(t), before=t)
                    else:
                        project(t)
                over_tiles(act, ph, head, body)

            ffn0(0)
            barrier(act, 1)
            attention0()
            barrier(act, 2)
            ffn0(2)
            barrier(act, 3)
            ffn1(3)
            barrier(act, 4)
            attention1()
            barrier(act, 5)
            ffn1(5)
            barrier(act, 6)

        @block.vector
        def _(dve):
            def copy(o, i):
                return dve.tensor_copy(o, i)

            def sub(o, a, b):
                return dve.tensor_tensor(o, a, b, ALU.subtract)

            once = Chain(dve, sem("dve_once"), 0)

            def unstage(n, pieces):
                cols = (staged + list(views["staged_late"]))[n][1]
                src = (stage[n % 2] if n < len(staged) else stage_l[n - len(staged)])[:, 0:cols]
                dve.wait_ge(w_in, 16 * max(n + 1, 2))
                last = once.step(copy(pieces[0], src))
                if len(pieces) == 2:
                    once.settle()
                    last = once.step(sub(pieces[1], src, pieces[0].bitcast(F32)))
                once.settle()
                dve.sem_inc(stage_free, 1)

            def flat(ap):
                dims = "abcd"[:len(ap.shape) - 1]
                return ap if len(ap.shape) == 2 else ap.rearrange(f"p {' '.join(dims)} -> p ({' '.join(dims)})")

            def x_block(ph, t, b):
                return x[:, bass.ds((t - FIRST[ph]) * BLK + b, 1), :]

            def x_tile(ph, t):
                return x[:, bass.ds((t - FIRST[ph]) * BLK, BLK), :]

            def normalise(ph, t, part):
                if part == 0:
                    if ph > 0:
                        dve.wait_ge(sig(ph - 1, "x_done"), (t - FIRST[ph] + FIRST[ph - 1]) * 4 + 4)
                    for b in range(BLK):
                        last = dve.bn_stats(stats[:, b, :], x_block(ph, t, b))
                    last.then_inc(sig(ph, "stats"), 1)
                    pass_wait(dve, sig(ph, "stats"), t + 1)
                    for b in range(BLK):
                        last = dve.bn_aggr(meanvar[:, b, :], stats[:, b, :])
                    last.then_inc(sig(ph, "meanvar"), 1)
                else:
                    dve.wait_ge(sig(ph, "rstd"), t + 1)
                    for b in range(BLK):
                        last = dve.tensor_scalar(xn[:, b, :], x_block(ph, t, b),
                                                 meanvar[:, b, 0:1], rstd[:, b:b + 1],
                                                 ALU.subtract, ALU.mult)
                    last.then_inc(sig(ph, "xn"), 1)

            def x_low(ph, t, p):
                dve.wait_ge(sig(ph, "x_hi"), t + 1)
                sub(xnT_hl[p][:, 1, :], xnT[:], xnT_hl[p][:, 0, :].bitcast(F32)).then_inc(sig(ph, "x_lo"), 1)


            def bias_parts():
                dve.wait_ge(bias_in, 16 * 6)
                resid = bias_f[:]
                for part in range(3):
                    once.step(copy(bias_p[:, part], resid))
                    once.settle()
                    if part < 2:
                        once.step(sub(bias_r[:, part], resid, bias_p[:, part]))
                        once.settle()
                        resid = bias_r[:, part]
                for k in range(2):
                    once.step(dve.tensor_scalar(bias_r[:, 0, k], bias_p[:, 0, k], small[:, 3 * k:3 * k + 1],
                                                None, ALU.mult))
                    once.settle()
                    once.step(dve.scalar_tensor_tensor(out=bias_r[:, 1, k], in0=bias_p[:, 1, k],
                                                       scalar=small[:, 3 * k + 1:3 * k + 2],
                                                       in1=bias_r[:, 0, k], op0=ALU.mult, op1=ALU.add))
                    once.settle()
                    once.step(dve.scalar_tensor_tensor(out=bias_m[:, k], in0=bias_p[:, 2, k],
                                                       scalar=small[:, 3 * k + 2:3 * k + 3],
                                                       in1=bias_r[:, 1, k], op0=ALU.mult, op1=ALU.add))
                once.step(dve.tensor_scalar(ones3[:], ones3[:], small[:, 11:12], None, ALU.add))
                once.settle()
                dve.sem_inc(setup, 1)

            def attention0_weights():
                dve.wait_ge(consts, 16 * 6)
                once.step(dve.tensor_tensor(temp_ind[:], temp_b[:], small[:, 16:16 + HEADS], ALU.mult))
                once.step(copy(qkvT_hl[:, 0], qkv_f[:, 0]))
                once.settle()
                once.step(sub(qkvT_hl[:, 1], qkv_f[:, 0], qkvT_hl[:, 0].bitcast(F32)))
                once.settle()

            def ffn0(ph):
                rc = Chain(dve, sig(ph, "route_steps"), 8)
                ac = Chain(dve, sig(ph, "add_steps"), BLK * E0)

                def route(t, p):
                    rc.tile(t)
                    dve.wait_ge(sig(ph, "lg"), t + 1)
                    lg = ps[:, SM, 0:BLK * E0].rearrange("p (b e) -> p b e", e=E0)
                    bc = [P, BLK, E0]
                    rc.step(dve.tensor_tensor(logit[:], lg, gate_b[:].unsqueeze(1).broadcast_to(bc), ALU.add))
                    rc.settle()
                    rc.step(dve.tensor_reduce(best[:], logit[:], AXX, ALU.max))
                    rc.settle()
                    rc.step(dve.tensor_tensor(equal[:], logit[:], best[:].unsqueeze(2).broadcast_to(bc),
                                              ALU.is_equal))
                    rc.settle()
                    rc.step(dve.tensor_tensor(equal[:], equal[:], small[:, 6:10].unsqueeze(1).broadcast_to(bc),
                                              ALU.mult))
                    rc.settle()
                    rc.step(dve.tensor_reduce(first[:], equal[:], AXX, ALU.max))
                    rc.settle()
                    rc.step(dve.tensor_tensor(logit[:], equal[:], first[:].unsqueeze(2).broadcast_to(bc),
                                              ALU.is_equal))
                    rc.settle()
                    rc.step(dve.tensor_scalar(half_hot[p][:], logit[:], 0.5, None, ALU.mult))
                    for k in range(3):
                        last = copy(onehot[:, :, E0 * k:E0 * k + E0], logit[:])
                    rc.step(last)
                    rc.settle()
                    dve.sem_inc(sig(ph, "hot"), 1)

                def masked(t, p, e):
                    dve.wait_ge(sig(ph, "mask"), t * E0 + e + 1)
                    dve.tensor_tensor(x_masked[p][:, e], xnT_hl[p][:].bitcast(F32),
                                      wide(MASK + e % 2).unsqueeze(1).broadcast_to([P, 2, SEQ]),
                                      ALU.mult).then_inc(sig(ph, "x_masked"), 1)

                def g_low(t, fb):
                    dve.wait_ge(sig(ph, "g_hi"), t * FB0 + fb + 1)
                    sub(g_lo[:, fb], g32[:, fb], g_hi[:, fb].bitcast(F32)).then_inc(sig(ph, "g_lo"), 1)

                def add_y(t, p, tb):
                    dve.wait_ge(sig(ph, "y"), t * BLK + tb + 1)
                    xt = x_block(ph, t, tb)
                    for e in range(E0):
                        last = dve.scalar_tensor_tensor(
                            out=xt, in0=ps[:, Y0 + tb % 2, e * D:e * D + D].unsqueeze(1),
                            scalar=half_hot[p][:, tb, e:e + 1],
                            in1=xt, op0=ALU.mult, op1=ALU.add)
                        ac.step(last)
                        ac.settle()
                    dve.sem_inc(sig(ph, "x_done"), 1)

                def head(t, p):
                    if ph == 0:
                        dve.wait_ge(x_first, 16)
                    normalise(ph, t, 0)
                    normalise(ph, t, 1)
                    if ph == 0:
                        dve.wait_ge(early_in, 16 * 4)
                        dve.wait_ge(setup, 2)
                        once.step(copy(ident_b[:], ident[:]))
                        once.settle()
                    x_low(ph, t, p)
                    route(t, p)
                    if ph == 0:
                        unstage(0, (flat(sel_expert[:]),))
                        bias_parts()
                        unstage(1, (flat(w1_hl[:, 0]), flat(w1_hl[:, 1])))
                    for e in range(E0):
                        masked(t, p, e)
                    if ph == 0:
                        unstage(2, (flat(w2_hl[:, 0]), flat(w2_hl[:, 1])))

                def body(t, p, more):
                    n, q = t + 1, 1 - p
                    ac.tile(t)
                    if more:
                        if ph == 0 and p == 1:
                            dve.wait_ge(x_rest, 16)
                        normalise(ph, n, 0)
                        normalise(ph, n, 1)
                    g_low(t, 0)
                    g_low(t, 1)
                    g_low(t, 2)
                    if more:
                        x_low(ph, n, q)
                    g_low(t, 3)
                    if more:
                        route(n, q)
                    for tb in range(BLK):
                        if more and tb == BLK - 1:
                            masked(n, q, 3)
                        add_y(t, p, tb)
                        if more and tb == 1:
                            masked(n, q, 0)
                            masked(n, q, 1)
                        if more and tb == 2:
                            masked(n, q, 2)
                over_tiles(dve, ph, head, body)

            def ffn1(ph):
                m = ffn1_mem
                rc = Chain(dve, sig(ph, "route_steps"), 11)

                def top(t, stage):
                    if stage == 0:
                        rc.tile(t)
                        dve.wait_ge(sig(ph, "lg"), t + 1)
                        rc.step(copy(m["logit"][:], rows4(SM)[:, :, 0:E1]))
                        rc.settle()
                        dve.sem_inc(sig(ph, "logit"), 1)
                        for b in range(BLK):
                            last = dve.max(m["top8"][:, b], m["logit"][:, b])
                        rc.step(last)
                    if stage == 1:
                        rc.settle()
                        rc.step(dve.memset(m["top8"][:, :, TOP1:8], BIG))
                        rc.settle_alone()
                        for b in range(BLK):
                            last = dve.match_replace(m["taken"][:, b], m["top8"][:, b], m["logit"][:, b], -BIG)
                        rc.step(last)
                    if stage == 2:
                        rc.settle()
                        rc.step(dve.tensor_tensor(m["gate"][:], m["taken"][:], m["logit"][:], ALU.is_lt))
                        rc.settle()
                        dve.wait_ge(sig(ph, "sigm"), t + 1)
                        rc.step(dve.tensor_tensor(m["gate"][:], m["gate"][:], m["sig"][:], ALU.mult))
                        gate_part(0)
                    if stage == 3:
                        gate_part(1)
                        gate_part(2)
                        rc.settle()
                        dve.sem_inc(sig(ph, "gates"), 1)

                def gate_part(part):
                    rest = [m["gate"][:], m["rest"][:, 0], m["rest"][:, 1]]
                    to = m["parts"][:, :, E1 * part:E1 * part + E1]
                    rc.settle()
                    rc.step(copy(to, rest[part]))
                    if part < 2:
                        rc.settle()
                        rc.step(sub(rest[part + 1], rest[part], to))

                def low(t, fb):
                    if fb not in POOL_FB:
                        dve.wait_ge(sig(ph, "hi"), t * FB1 + fb + 1)
                        sub(m["lo"][:, fb % RING1], m["m32"][:, fb % RING1], m["hi"][:, fb % RING1].bitcast(F32))\
                            .then_inc(sig(ph, "lo_dve"), 1)

                def add_y(t):
                    dve.wait_ge(sig(ph, "y_rows"), t + 1)
                    dve.scalar_tensor_tensor(out=x_tile(ph, t), in0=rows4(TR), scalar=0.5, in1=x_tile(ph, t),
                                             op0=ALU.mult, op1=ALU.add).then_inc(sig(ph, "x_done"), 4)

                def step(t, p, fb, more, before=None):
                    if more and fb in (LEAD, LEAD + 1):
                        normalise(ph, t + 1, fb - LEAD)
                    dve.wait_ge(sig(ph, "relu"), t * FB1 + fb + 1)
                    dve.tensor_tensor(m["m32"][:, fb % RING1], m["relu"][:, fb % 4], wide(G1 + fb % 2),
                                      ALU.mult).then_inc(sig(ph, "m"), 1)
                    if fb > 0:
                        low(t, fb - 1)
                    elif before is not None:
                        low(before, FB1 - 1)
                    if more and fb in (9, 10, 11, 12):
                        top(t + 1, fb - 9)
                    if more and fb == 13:
                        x_low(ph, t + 1, 1 - p)

                def head(t, p):
                    normalise(ph, t, 0)
                    normalise(ph, t, 1)
                    x_low(ph, t, p)
                    for stage_ in range(4):
                        top(t, stage_)
                    for fb in range(LEAD):
                        step(t, p, fb, True)

                def body(t, p, more):
                    for fb in range(LEAD, FB1):
                        step(t, p, fb, more)
                    if more:
                        for fb in range(LEAD):
                            step(t + 1, 1 - p, fb, True, before=t)
                    else:
                        low(t, FB1 - 1)
                    add_y(t)
                over_tiles(dve, ph, head, body)

            def attention0():
                ph = 1
                hc = Chain(dve, sig(ph, "head_steps"), 7)
                bc_ = Chain(dve, sig(ph, "body_steps"), 5)

                def scaled(t):
                    hc.n = 0
                    hc.tile(t)
                    dve.wait_ge(sig(ph, "wsq"), t + 1)
                    hc.step(dve.tensor_scalar(inv2[:], norm2[:], 1e-24, None, ALU.max))
                    hc.settle()
                    hc.step(dve.reciprocal(inv2[:], inv2[:]))
                    hc.settle()
                    hc.step(dve.tensor_scalar(norm_ind[:], temp_ind[:], inv2[:], None, ALU.mult))
                    hc.settle()
                    dve.sem_inc(sig(ph, "norm_ind"), 1)

                bc = [P, BLK, HEADS]

                def shifted(t):
                    dve.wait_ge(sig(ph, "s"), t + 1)
                    s = ps[:, SC, 0:BLK * HEADS].rearrange("p (b h) -> p b h", h=HEADS)
                    hc.step(dve.tensor_reduce(smax[:], s, AXX, ALU.max))
                    hc.settle()
                    dve.tensor_tensor(sexp[:], s, smax[:].unsqueeze(2).broadcast_to(bc), ALU.subtract)\
                       .then_inc(sig(ph, "s_shift"), 1)

                def softmax(t, p):
                    dve.wait_ge(sig(ph, "s_exp"), t + 1)
                    hc.step(dve.tensor_reduce(ssum[:], sexp[:], AXX, ALU.add))
                    hc.settle()
                    hc.step(dve.reciprocal(ssum[:], ssum[:]))
                    hc.settle()
                    hc.step(dve.tensor_tensor(pi[p][:, :, 0:HEADS], sexp[:],
                                              ssum[:].unsqueeze(2).broadcast_to(bc), ALU.mult))
                    hc.settle()
                    dve.sem_inc(sig(ph, "pi"), 1)

                def minus_attn(t, k):
                    bc_.n = 0
                    bc_.tile(t)
                    dve.wait_ge(sig(ph, "pi_sum"), t + 1)
                    bc_.step(dve.tensor_tensor_reduce(out=prod[:], in0=wsq[k][:], in1=pi_rows[:], scale=1.0,
                                                      scalar=0.0, op0=ALU.mult, op1=ALU.add,
                                                      accum_out=dots[:, 0:1]))
                    bc_.step(dve.tensor_scalar(dots[:, 1:2], pi_sum[:], 1e-8, -1.0, ALU.add, ALU.mult))
                    bc_.settle()
                    bc_.step(dve.reciprocal(dots[:, 2:3], dots[:, 1:2]))
                    bc_.settle()
                    bc_.step(dve.tensor_scalar(dots[:, 3:4], dots[:, 0:1], dots[:, 2:3], -1.0,
                                               ALU.mult, ALU.add))
                    bc_.settle()
                    bc_.step(dve.reciprocal(dots[:, 0:1], dots[:, 3:4]))
                    bc_.settle()

                def attended(t, k):
                    dve.wait_ge(sig(ph, "w32"), t + 1)
                    dve.scalar_tensor_tensor(out=outT[:], in0=w32[k][:], scalar=dots[:, 0:1], in1=pi_rows[:],
                                             op0=ALU.mult, op1=ALU.mult).then_inc(sig(ph, "outT"), 1)

                def add_y(t):
                    dve.wait_ge(sig(ph, "biased"), t + 1)
                    dve.wait_ge(sig(ph, "y"), t + 1)
                    dve.tensor_tensor(x_tile(ph, t), x_tile(ph, t), rows4(YA), ALU.add)\
                       .then_inc(sig(ph, "x_done"), 4)

                def step(t, k, here):
                    if here(1):
                        scaled(t + 1)
                    if here(2):
                        normalise(ph, t + 2, 1)
                    if here(1):
                        shifted(t + 1)
                    if here(-1):
                        add_y(t - 1)
                    if here(1):
                        softmax(t + 1, (k + 1) % 2)
                    if here(2):
                        x_low(ph, t + 2, k % 2)
                    if here(0):
                        minus_attn(t, k)
                    if here(3):
                        normalise(ph, t + 3, 0)
                    if here(0):
                        attended(t, k)
                normalise(ph, 0, 0)
                three_deep(dve, step)

            def attention1_weights():
                dve.wait_ge(sig(4, "tables"), 16 * 5)
                unstage(6, (flat(stack_sel[:]),))
                qk_stage = stage_l[1][:, 0:4 * P].rearrange("p (a b) -> p a b", a=4)
                dve.wait_ge(w_in, 16 * 8)
                once.step(copy(w_qk[:, :, 0], qk_stage))
                once.settle()
                once.step(sub(w_qk[:, :, 1], qk_stage, w_qk[:, :, 0].bitcast(F32)))
                once.step(copy(ident_r[:], ident[:]))
                once.settle()
                dve.sem_inc(sig(4, "weights"), 1)

            def attention1():
                ph = 4

                def rotary(t, i):
                    dve.wait_ge(sig(ph, "qk"), t * 4 + i + 1)
                    if i == 2:
                        dve.wait_ge(sig(ph, "rope_sum"), t * 2 + 1)
                    dve.tensor_tensor(rope[:, i % 2], wide(MISC), (cos_t, sin_t)[i % 2][:],
                                      ALU.mult).then_inc(sig(ph, "qk_read"), 1)

                def maxima(t, g, j, blocks=range(BLK)):
                    for b in blocks:
                        dve.wait_ge(sig(ph, "s1"), (t * GROUPS + g) * 16 + 4 * j + b + 1)
                        dve.tensor_reduce(qmax[:, g % 2, j, b:b + 1], wide(PASS1 + b % 2), AXX,
                                          ALU.max).then_inc(sig(ph, "qmax"), 1)

                def minus_max(t, g):
                    dve.wait_ge(sig(ph, "qmax"), (t * GROUPS + g + 1) * 16)
                    to = shift[:, g % 2].rearrange("p b (j r) -> p b j r", r=32)[:, :, :, 3 * HD]
                    dve.tensor_scalar(to, qmax[:, g % 2].rearrange("p j b -> p b j"), -1.0, None,
                                      ALU.mult).then_inc(sig(ph, "shift"), 1)

                def low(t, h):
                    dve.wait_ge(sig(ph, "prob"), t * 2 * HEADS + 2 * h + 1)
                    s, kb = h % HP, slice(0, BLK - POOL_KB)
                    sub(prob_lo[:, s, kb], prob[:, s, kb], prob_hi(s)[:, kb]).then_inc(sig(ph, "lo_dve"), 1)

                def output(t, g):
                    dve.wait_ge(sig(ph, "pv"), (t * GROUPS + g + 1) * HPG)
                    o = ps[:, OB, 0:HPG * BLK * VC].rearrange("p (n c) -> p n c", c=VC)
                    dve.tensor_reduce(o_sum[:], o[:, :, 0:3 * HD].rearrange("p n (k d) -> p n d k", k=3),
                                      AXX, ALU.add)
                    dve.reciprocal(o_rcp[:], o[:, :, 3 * HD]).then_inc(sig(ph, "o_read"), 1)
                    dve.wait_ge(sig(ph, "o_read"), t * GROUPS + g + 1)
                    to = o_all[:].rearrange("p b (h d) -> p h b d", d=HD)[:, HPG * g:HPG * g + HPG]
                    src = o_sum[:].rearrange("p (j b) d -> p j b d", j=HPG)
                    rcp = o_rcp[:].rearrange("p (j b) -> p j b", j=HPG)
                    last = dve.tensor_tensor(to, src, rcp.unsqueeze(3).broadcast_to([P, HPG, BLK, HD]), ALU.mult)
                    if g == GROUPS - 1:
                        last.then_inc(sig(ph, "o_all"), 1)

                def head(t, p):
                    normalise(ph, t, 0)
                    normalise(ph, t, 1)
                    attention1_weights()
                    for i in range(4):
                        rotary(t, i)
                    for h in range(AHEAD):
                        maxima(t, h // HPG, h % HPG)
                        if h == HPG - 1:
                            minus_max(t, 0)
                    for h in range(EARLY):
                        step(t, p, h, True)

                def add_projected(t):
                    dve.wait_ge(sig(ph, "y"), t + 1)
                    dve.wait_ge(sig(ph, "biased"), t + 1)
                    dve.tensor_tensor(x_tile(ph, t), x_tile(ph, t), rows4(MISC), ALU.add)\
                       .then_inc(sig(ph, "x_done"), 4)

                def step(t, p, h, more, before=None):
                    n = t + 1
                    if h == 1 and more:
                        normalise(ph, n, 0)
                    if h == 2 and more:
                        normalise(ph, n, 1)
                    ahead = h + AHEAD
                    if ahead < HEADS or more:
                        maxima(t + ahead // HEADS, ahead % HEADS // HPG, ahead % HPG, (0, 1))
                    if h in (6, 7, 8) and more:
                        rotary(n, {6: 0, 7: 2, 8: 3}[h])
                    if h >= 1:
                        low(t, h - 1)
                    elif before is not None:
                        low(before, HEADS - 1)
                    if h == 6 and more:
                        rotary(n, 1)
                    if ahead < HEADS or more:
                        maxima(t + ahead // HEADS, ahead % HEADS // HPG, ahead % HPG, (2, 3))
                    if h % HPG == 0 and h > 0:
                        output(t, h // HPG - 1)
                    if h == 0 and before is not None:
                        output(before, GROUPS - 1)
                    if h == 2 and before is not None:
                        add_projected(before)
                    if ahead % HPG == HPG - 1 and (ahead < HEADS or more):
                        minus_max(t + ahead // HEADS, ahead % HEADS // HPG)

                def body(t, p, more):
                    for h in range(EARLY, HEADS):
                        step(t, p, h, more)
                    if more:
                        for h in range(EARLY):
                            step(t + 1, 1 - p, h, two_more(t), before=t)
                    else:
                        low(t, HEADS - 1)
                        output(t, GROUPS - 1)
                        add_projected(t)
                over_tiles(dve, ph, head, body)

            ffn0(0)
            attention0_weights()
            unstage(3, (flat(sel_gate[:]),))
            unstage(4, (keys_hl[:, 0], keys_hl[:, 1]))
            unstage(5, (flat(vals_hl[:, 0]), flat(vals_hl[:, 1])))
            barrier(dve, 1)
            dve.wait_ge(sig(1, "zeroed"), 1)
            attention0()
            barrier(dve, 2)
            ffn0(2)
            barrier(dve, 3)
            ffn1(3)
            barrier(dve, 4)
            attention1()
            barrier(dve, 5)
            ffn1(5)
            barrier(dve, 6)

        @block.tensor
        def _(pe):
            def three(dst, w_hi, w_lo, x_hi, x_lo, start=True, stop=True):
                pe.matmul(dst, w_hi, x_hi, start=start, stop=False)
                pe.matmul(dst, w_hi, x_lo, start=False, stop=False)
                return pe.matmul(dst, w_lo, x_hi, start=False, stop=stop)

            def transpose_in(ph, t, bank):
                pe.wait_ge(sig(ph, "xn"), t + 1)
                for b in range(BLK):
                    last = pe.transpose(rows4(bank)[:, b], xn[:, b], ident[:])
                last.then_inc(sig(ph, "tr"), 1)

            def route(ph, t, weights, n):
                pe.wait_ge(sig(ph, "xnT"), t + 1)
                for b in range(BLK):
                    dst = ps[:, SM, b * E0:b * E0 + E0] if n == E0 else rows4(SM)[:, b, 0:n]
                    last = pe.matmul(dst, xnT[:, b * P:b * P + P], weights, start=True, stop=True)
                last.then_inc(sig(ph, "lg"), 1)

            def ffn0(ph):
                def hotT(t):
                    pe.wait_ge(sig(ph, "hot"), t + 1)
                    dst = wide(SM, dt=BF16)[0:3 * E0, 512:1024]
                    for b in range(BLK):
                        last = pe.transpose(dst[:, b * P:b * P + P], onehot[:, b], ident_b[:])
                    last.then_inc(sig(ph, "hotT"), 1)

                def mask(t, p, e):
                    if e == 0:
                        pe.wait_ge(sig(ph, "onehotT"), t + 1)
                    if e >= 2:
                        pe.wait_ge(sig(ph, "x_masked"), t * E0 + e - 1)
                    pe.matmul(wide(MASK + e % 2), sel_expert[:, e], onehotT[p][:], start=True, stop=True)\
                      .then_inc(sig(ph, "mask"), 1)

                def up(t, p, fb):
                    dst = wide(H0 + fb % 2)
                    if fb >= 2:
                        pe.wait_ge(sig(ph, "gelu"), t * FB0 + fb - 1)
                    pe.matmul(dst, bias_m[:, 0, fb * P:fb * P + P], onehotT[p][:], start=True, stop=False)
                    for e in range(E0):
                        if fb == 0:
                            pe.wait_ge(sig(ph, "x_masked"), t * E0 + e + 1)
                        c = slice(fb * P, fb * P + P)
                        last = three(dst, w1_hl[:, 0, e, c], w1_hl[:, 1, e, c], x_masked[p][:, e, 0],
                                     x_masked[p][:, e, 1], start=False, stop=(e == E0 - 1))
                    last.then_inc(sig(ph, "h"), 1)

                def down(t, tb):
                    dst = wide(Y0 + tb % 2)
                    if tb >= 2:
                        pe.wait_ge(sig(ph, "x_done"), t * BLK + tb - 1)
                    if tb == 0:
                        pe.wait_ge(sig(ph, "g_lo"), t * FB0 + 1)
                    pe.matmul(dst, ones3[:], bias_m[:, 1], start=True, stop=False)
                    c = slice(tb * P, tb * P + P)
                    for fb in range(FB0):
                        if tb == 0 and fb > 0:
                            pe.wait_ge(sig(ph, "g_lo"), t * FB0 + fb + 1)
                        pe.matmul(dst, g_hi[:, fb, c], w2_hl[:, 0, fb], start=False, stop=False)
                        pe.matmul(dst, g_hi[:, fb, c], w2_hl[:, 1, fb], start=False, stop=False)
                        last = pe.matmul(dst, g_lo[:, fb, c], w2_hl[:, 0, fb], start=False,
                                         stop=(fb == FB0 - 1))
                    last.then_inc(sig(ph, "y"), 1)

                def head(t, p):
                    if ph == 0:
                        pe.wait_ge(early_in, 16 * 4)
                    transpose_in(ph, t, TR)
                    route(ph, t, gate_w[:], E0)
                    hotT(t)
                    if ph == 0:
                        pe.wait_ge(stage_free, 1)
                    for e in range(E0):
                        mask(t, p, e)

                def body(t, p, more):
                    n, q = t + 1, 1 - p
                    if ph == 0:
                        pe.wait_ge(setup, 3)
                        pe.wait_ge(stage_free, 2)
                    for fb in range(FB0):
                        up(t, p, fb)
                        if more and fb == 2:
                            transpose_in(ph, n, TR)
                        if more and fb == 3:
                            route(ph, n, gate_w[:], E0)
                    if ph == 0:
                        pe.wait_ge(stage_free, 3)
                    for tb in range(BLK):
                        down(t, tb)
                        if more and tb == 0:
                            hotT(n)
                        if more and tb == 1:
                            mask(n, q, 0)
                            mask(n, q, 1)
                        if more and tb >= 2:
                            mask(n, q, tb)
                over_tiles(pe, ph, head, body)

            def ffn1(ph):
                m = ffn1_mem

                def gateT(t, p):
                    pe.wait_ge(sig(ph, "gates"), t + 1)
                    for b in range(BLK):
                        last = pe.transpose(wide(TR, dt=BF16)[0:3 * E1, b * P:b * P + P], m["parts"][:, b],
                                            ident_b[:])
                    last.then_inc(sig(ph, "gT"), 1)

                def up(t, p, fb):
                    first = isinstance(t, int) and t == 0
                    if not (first and fb < h1_since[fb]):
                        pe.wait_ge(sig(ph, "relu"), t * FB1 + fb - h1_since[fb] + 1)
                    if fb == 0:
                        pe.wait_ge(sig(ph, "x_lo"), t + 1)
                    c = slice(fb * P, fb * P + P)
                    three(wide(h1_bank[fb]), keys_hl[:, 0, c], keys_hl[:, 1, c], xnT_hl[p][:, 0],
                          xnT_hl[p][:, 1])
                    if not (first and fb < 2):
                        pe.wait_ge(sig(ph, "m"), t * FB1 + fb - 1)
                    if fb == 0:
                        pe.wait_ge(sig(ph, "gateT"), t + 1)
                    pe.matmul(wide(G1 + fb % 2), sel_gate[:, fb], m["gateT"][p][:], start=True, stop=True)\
                      .then_inc(sig(ph, "h"), 1)

                def down(t, fb):
                    k = sum(f in POOL_FB for f in range(fb + 1))
                    if fb in POOL_FB:
                        pe.wait_ge(sig(ph, "lo_pool"), t * len(POOL_FB) + k)
                    else:
                        pe.wait_ge(sig(ph, "lo_dve"), t * (FB1 - len(POOL_FB)) + fb + 1 - k)
                    s = fb % RING1
                    last = three(wide(Y1), vals_hl[:, 0, fb], vals_hl[:, 1, fb], m["hi"][:, s], m["lo"][:, s],
                                 start=(fb == 0), stop=(fb == FB1 - 1))
                    if fb == FB1 - 1:
                        last.then_inc(sig(ph, "y"), 1)

                def step(t, p, fb, more, before=None):
                    if before is not None and fb == LEAD - 1:
                        down(before, fb - LEAD + FB1)
                    up(t, p, fb)
                    if fb >= LEAD:
                        down(t, fb - LEAD)
                    elif before is not None and fb < LEAD - 1:
                        down(before, fb - LEAD + FB1)
                    if more and fb == 7:
                        transpose_in(ph, t + 1, TR)
                    if more and fb == 9:
                        route(ph, t + 1, router1[:], E1)
                    if more and fb == 15:
                        gateT(t + 1, 1 - p)

                def y_rows(t):
                    pe.wait_ge(sig(ph, "yT"), t + 1)
                    for b in range(BLK):
                        last = pe.transpose(rows4(TR)[:, b], m["yT"][:, b * P:b * P + P], ident[:])
                    last.then_inc(sig(ph, "y_rows"), 1)

                def head(t, p):
                    transpose_in(ph, t, TR)
                    route(ph, t, router1[:], E1)
                    gateT(t, p)
                    for fb in range(LEAD):
                        step(t, p, fb, True)

                def body(t, p, more):
                    for fb in range(LEAD, FB1):
                        step(t, p, fb, more)
                    for fb in range(LEAD):
                        if more:
                            step(t + 1, 1 - p, fb, True, before=t)
                        else:
                            down(t, fb - LEAD + FB1)
                    y_rows(t)
                over_tiles(pe, ph, head, body)

            def attention0():
                ph = 1

                def step(t, k, here):
                    if here(0):
                        pe.wait_ge(sig(ph, "pi"), t + 1)
                        for b in range(BLK):
                            last = pe.transpose(rows4(PT)[:, b], pi[k % 2][:, b], ident[:])
                        last.then_inc(sig(ph, "piT"), 1)
                    if here(1):
                        pe.wait_ge(sig(ph, "norm_ind"), t + 2)
                        for b in range(BLK):
                            last = pe.matmul(ps[:, SC, b * HEADS:b * HEADS + HEADS],
                                             wsq[(k + 1) % 4][:, b * P:b * P + P], norm_ind[:],
                                             start=True, stop=True)
                        last.then_inc(sig(ph, "s"), 1)
                    if here(-1):
                        pe.wait_ge(sig(ph, "outT"), t)
                        for b in range(BLK):
                            last = pe.matmul(rows4(YA)[:, b], outT[:, b * P:b * P + P], qkv_f[:, 1],
                                             start=True, stop=True)
                        last.then_inc(sig(ph, "y"), 1)
                    if here(2):
                        transpose_in(ph, t + 2, TR)
                    if here(0):
                        pe.wait_ge(sig(ph, "piT_sb"), t + 1)
                        pe.matmul(wide(PR), head_rows[:], piT[:], start=True, stop=True)\
                          .then_inc(sig(ph, "pi_rows"), 1)
                    if here(2):
                        pe.wait_ge(sig(ph, "x_lo"), t + 3)
                        xh = xnT_hl[k % 2]
                        three(wide(WT), qkvT_hl[:, 0], qkvT_hl[:, 1], xh[:, 0], xh[:, 1])\
                            .then_inc(sig(ph, "w"), 1)
                three_deep(pe, step)

            def attention1():
                ph = 4

                def queries(t, g, p, name):
                    s = stack_sel[:, g]
                    if g == 0:
                        pe.wait_ge(sig(ph, "qk_hl"), 2 * t + 2)
                    pe.matmul(wide(MISC), s[:, 0], qk_hl[p][:, 1, 0], start=True, stop=False)
                    last = pe.matmul(wide(MISC), s[:, 1], qk_hl[p][:, 1, 1], start=False, stop=True)
                    if name == "qsh":
                        for b in range(BLK):
                            last = pe.matmul(rows4(MISC)[:, b], shift[:, g % 2, b], ident_r[:], start=False,
                                             stop=True, skip_group_check=True)
                    last.then_inc(sig(ph, name), 1)

                def keys(t, g, p):
                    s = stack_sel[:, g]
                    if g == 0:
                        pe.wait_ge(sig(ph, "qk_hl"), 2 * t + 1)
                    pe.matmul(wide(MISC), s[:, 2], qk_hl[p][:, 0, 0], start=True, stop=False)
                    pe.matmul(wide(MISC), s[:, 3], qk_hl[p][:, 0, 1], start=False, stop=True)\
                      .then_inc(sig(ph, "ks"), 1)
                def pass1(t, g, j, blocks=range(BLK)):
                    if j == 0 and 0 in blocks:
                        pe.wait_ge(sig(ph, "qs_sb"), t * GROUPS + g + 1)
                    for b in blocks:
                        if not (isinstance(t, int) and t == g == 0 and 4 * j + b < 2):
                            pe.wait_ge(sig(ph, "qmax"), (t * GROUPS + g) * 16 + 4 * j + b - 1)
                        pe.matmul(wide(PASS1 + b % 2), q_st[:, g % 2, b * P:b * P + P], k_pad[:, HPG * g + j],
                                  start=True, stop=True).then_inc(sig(ph, "s1"), 1)

                def pass2(t, h, half, first=False):
                    if h % HPG == 0 and half == 0:
                        pe.wait_ge(sig(ph, "qsh_sb"), t * GROUPS + h // HPG + 1)
                    for b in (2 * half, 2 * half + 1):
                        if b % 2 == 0 and not first:
                            pe.wait_ge(sig(ph, "prob"), t * 2 * HEADS + 2 * h - 1 + b // 2)
                        last = pe.matmul(wide(PASS2 + b), k_pad[:, h, b * P:b * P + P],
                                         q_sh[:, (h // HPG) % 2], start=True, stop=True)
                        if b % 2:
                            last.then_inc(sig(ph, "st"), 1)

                def values(t, h, p):
                    pe.wait_ge(sig(ph, "lo_pool"), t * HEADS + h + 1)
                    pe.wait_ge(sig(ph, "lo_dve"), t * HEADS + h + 1)
                    g, s = h // HPG, h % HP
                    if h % HPG == 0 and g > 0:
                        pe.wait_ge(sig(ph, "o_read"), t * GROUPS + g)
                    if h == 0:
                        pe.wait_ge(sig(ph, "v_parts"), t + 1)
                    hi = prob_hi(s)
                    for qb in range(BLK):
                        o0 = ((h % HPG) * BLK + qb) * VC
                        dst = ps[:, OB, o0:o0 + VC]
                        c = slice(qb * P, qb * P + P)
                        for kb in range(BLK):
                            v = v_parts[p][:, kb, h]
                            pe.matmul(dst, hi[:, kb, c], v, start=(kb == 0), stop=False)
                            last = pe.matmul(dst, prob_lo[:, s, kb, c], v, start=False, stop=(kb == BLK - 1))
                    last.then_inc(sig(ph, "pv"), 1)

                def head_v(t, p):
                    pe.wait_ge(sig(ph, "x_hi"), t + 1)
                    for b in range(BLK):
                        last = pe.matmul(rows4(MISC)[:, b], xnT[:, b * P:b * P + P], w_v[:], start=True,
                                         stop=True)
                    last.then_inc(sig(ph, "v"), 1)

                def head_qk(t, p, i):
                    if i == 0:
                        pe.wait_ge(sig(ph, "x_lo"), t + 1)
                    three(wide(MISC), w_qk[:, i, 0], w_qk[:, i, 1], xnT_hl[p][:, 0], xnT_hl[p][:, 1])\
                        .then_inc(sig(ph, "qk"), 1)

                def bank_read(name, count):
                    pe.wait_ge(sig(ph, name), count)

                def attended(t):
                    pe.wait_ge(sig(ph, "o_all"), t + 1)
                    for b in range(BLK):
                        last = pe.transpose(rows4(MISC)[:, b], o_all[:, b], ident[:])
                    last.then_inc(sig(ph, "oT"), 1)

                def project(t):
                    pe.wait_ge(sig(ph, "oT_sb"), t + 1)
                    for b in range(BLK):
                        last = pe.matmul(rows4(MISC)[:, b], oT[:, b * P:b * P + P], w_o[:], start=True,
                                         stop=True)
                    last.then_inc(sig(ph, "y"), 1)

                def shifted(t, g, p):
                    pe.wait_ge(sig(ph, "shift"), t * GROUPS + g + 1)
                    queries(t, g, p, "qsh")

                def small_work(t, p, h, more, before):
                    n, q, g4 = t + 1, 1 - p, t * GROUPS
                    if h == 0:
                        bank_read("qsh_sb", g4 + 1)
                        keys(t, 2, p)
                    if h == 1:
                        bank_read("k_pad", g4 + 3)
                        queries(t, 2, p, "qs")
                    if h == 2 and before is not None:
                        project(before)
                    if h == 3:
                        bank_read("qs_sb", g4 + 3)
                        shifted(t, 1, p)
                    if h == 4:
                        if more:
                            bank_read("x_hi", n + 1)
                        else:
                            bank_read("qsh_sb", g4 + 2)
                        keys(t, 3, p)
                    if h == 5:
                        bank_read("k_pad", g4 + 4)
                        queries(t, 3, p, "qs")
                    if h == 6 and more:
                        bank_read("qk_read", n * 4 + 1)
                        head_qk(n, q, 1)
                    if h == 7:
                        if more:
                            bank_read("qk_read", n * 4 + 3)
                        else:
                            bank_read("qs_sb", g4 + 4)
                        shifted(t, 2, p)
                    if h == 9 and more:
                        bank_read("v_part", n * 2 + 1)
                        keys(n, 0, q)
                    if h == 10 and more:
                        bank_read("k_pad", n * GROUPS + 1)
                        queries(n, 0, q, "qs")
                    if h == 11:
                        if more:
                            bank_read("qs_sb", n * GROUPS + 1)
                        else:
                            bank_read("qsh_sb", g4 + 3)
                        shifted(t, 3, p)
                    if h == 12 and more:
                        bank_read("qsh_sb", g4 + 4)
                        keys(n, 1, q)
                    if h == 13 and more:
                        bank_read("k_pad", n * GROUPS + 2)
                        queries(n, 1, q, "qs")
                    if h == 15 and more:
                        bank_read("qs_sb", n * GROUPS + 2)
                        shifted(n, 0, q)

                def late_work(t, p, h, more, before):
                    n, q, g4 = t + 1, 1 - p, t * GROUPS
                    if h == 1 and before is not None:
                        bank_read("qs_sb", g4 + 3)
                        attended(before)
                    if h == 3 and more:
                        bank_read("qsh_sb", g4 + 2)
                        transpose_in(ph, n, MISC)
                    if h == 5 and more:
                        bank_read("qs_sb", g4 + 4)
                        head_qk(n, q, 0)
                    if h == 6 and more:
                        bank_read("qk_read", n * 4 + 2)
                        head_qk(n, q, 2)
                    if h == 7 and more:
                        bank_read("qsh_sb", g4 + 3)
                        head_qk(n, q, 3)
                    if h == 8 and more:
                        bank_read("qk_read", n * 4 + 4)
                        head_v(n, q)

                def step(t, p, h, more, before=None):
                    first = h == 0 and before is None
                    ahead = h + AHEAD
                    scores = ahead < HEADS or more
                    t1, g, j = t + ahead // HEADS, ahead % HEADS // HPG, ahead % HPG
                    pass2(t, h, 0, first)
                    small_work(t, p, h, more, before)
                    if scores:
                        pass1(t1, g, j, (2,))
                    pass2(t, h, 1, first)
                    if scores:
                        pass1(t1, g, j, (3,))
                    if h > 0:
                        values(t, h - 1, p)
                    elif before is not None:
                        values(before, HEADS - 1, 1 - p)
                    pass1_ahead(t, h + 1, more)
                    late_work(t, p, h, more, before)

                def pass1_ahead(t, h, more):
                    ahead = h + AHEAD
                    if ahead < HEADS or more:
                        pass1(t + ahead // HEADS, ahead % HEADS // HPG, ahead % HPG, (0, 1))

                def head(t, p):
                    transpose_in(ph, t, MISC)
                    pe.wait_ge(sig(ph, "weights"), 1)
                    head_v(t, p)
                    bank_read("v_part", 2 * t + 1)
                    head_qk(t, p, 0)
                    for i in range(1, 4):
                        bank_read("qk_read", t * 4 + i)
                        head_qk(t, p, i)
                    bank_read("qk_read", t * 4 + 4)
                    for g in range(2):
                        if g == 1:
                            bank_read("qs_sb", t * GROUPS + 1)
                        keys(t, g, p)
                        bank_read("k_pad", t * GROUPS + g + 1)
                        queries(t, g, p, "qs")
                    bank_read("qs_sb", t * GROUPS + 2)
                    for h in range(AHEAD):
                        if h == HPG:
                            shifted(t, 0, p)
                        pass1(t, h // HPG, h % HPG)
                    pe.wait_ge(sig(ph, "qsh_sb"), t * GROUPS + 1)
                    pass1_ahead(t, 0, True)
                    for h in range(EARLY):
                        step(t, p, h, True)

                def body(t, p, more):
                    for h in range(EARLY, HEADS):
                        step(t, p, h, more)
                    if more:
                        for h in range(EARLY):
                            step(t + 1, 1 - p, h, two_more(t), before=t)
                    else:
                        values(t, HEADS - 1, p)
                        attended(t)
                        project(t)
                over_tiles(pe, ph, head, body)

            ffn0(0)
            barrier(pe, 1)
            attention0()
            barrier(pe, 2)
            ffn0(2)
            barrier(pe, 3)
            ffn1(3)
            barrier(pe, 4)
            attention1()
            barrier(pe, 5)
            ffn1(5)
            barrier(pe, 6)


def kernel(**inputs):
    import concourse.bacc as _bacc
    from concourse.bass_utils import run_bass_kernel_spmd as _run

    def a(name):
        return np.asarray(inputs[name])

    qkv = a("L1_attn_w_qkv").reshape(D, 3, HEADS, HD // 2, 2)
    swapped = qkv[..., ::-1]
    w_qk = np.stack([qkv[:, 1], swapped[:, 1], qkv[:, 0], swapped[:, 0]], axis=1).reshape(D, 4 * P)
    data = {
        "x": a("L0_attn_x"), "gate_w": a("L0_ffn_Wg"), "gate_b": a("L0_ffn_bg"),
        "b1": a("L0_ffn_b1"), "b2": a("L0_ffn_b2").reshape(1, E0 * D),
        "W1": a("L0_ffn_W1").transpose(1, 0, 2).reshape(D, E0 * FF0),
        "W2": a("L0_ffn_W2").reshape(E0, FB0, P, D).transpose(2, 1, 0, 3).reshape(P, FB0 * E0 * D),
        "qkv_wT": a("L0_attn_qkv_w").T, "out_wT": a("L0_attn_out_w").T,
        "out_b0": a("L0_attn_out_b"), "temp": a("L0_attn_temp").reshape(HEADS),
        "selT": a("L1_ffn_expert_sel").T,
        "keys": a("L1_ffn_keys").transpose(1, 0, 2).reshape(D, E1 * FF1),
        "values": a("L1_ffn_values").reshape(FB1, P, D).transpose(1, 0, 2).reshape(P, FB1 * D),
        "w_qk": w_qk, "w_v": qkv[:, 2].reshape(D, P), "w_o": a("L1_attn_w_proj"),
        "out_b1": a("L1_attn_b_proj"),
    }
    data.update({f"c_{k}": v for k, v in token_constants().items()})
    nc = _bacc.Bacc("TRN2", target_bir_lowering=False, num_devices=1)
    arrays, d = {}, {}
    for name, v in data.items():
        v = np.ascontiguousarray(v)
        arrays[f"in_{name}"] = v
        d[name] = nc.dram_tensor(f"in_{name}", v.shape, mybir.dt.from_np(v.dtype), kind="ExternalInput").ap()
    out = nc.dram_tensor("out_0", (BATCH, SEQ, D), F32, kind="ExternalOutput").ap()
    const = {k[2:]: v for k, v in d.items() if k.startswith("c_")}
    weights = dict(
        gate_w=d["gate_w"], gate_b=d["gate_b"], b1=d["b1"], b2=d["b2"], router1=d["selT"],
        qkv_w=d["qkv_wT"], out_w=d["out_wT"], out_b0=d["out_b0"], temp=d["temp"],
        w_v=d["w_v"], w_o=d["w_o"], out_b1=d["out_b1"],
        staged=[
            (const["sel_expert"], E0 * P),
            (d["W1"], E0 * FF0),
            (d["W2"], FB0 * E0 * D),
            (const["sel_gate"], FB1 * P),
            (d["keys"], E1 * FF1),
            (d["values"], FB1 * D),
        ],
        staged_late=[(const["stack"], GROUPS * 4 * P), (d["w_qk"], 4 * P)],
    )
    macaron(nc, d["x"], weights, const, out)
    r = _run(nc, [arrays], core_ids=[0])
    return r.results[0]["out_0"]
```
